# Optimizing a Trainium2 kernel written in Bass

```python
import numpy as np
import jax
import jax.numpy as jnp

def _softmax(x, axis=-1):
    return jax.nn.softmax(x, axis=axis)

def _gelu(x):
    return jax.nn.gelu(x, approximate=True)

def _silu(x):
    return jax.nn.silu(x)

def _sigmoid(x):
    return jax.nn.sigmoid(x)

def _layernorm(x, axis=-1, eps=1e-05):
    m = jnp.mean(x, axis=axis, keepdims=True)
    v = jnp.var(x, axis=axis, keepdims=True)
    return (x - m) / jnp.sqrt(v + eps)

def _scatter_add(tgt, idx, src, axis=0):
    return tgt.at[idx].add(src)

def _segment_sum(src, seg, n):
    return jax.ops.segment_sum(src, seg, n)
kernel_name = 'mk_gnn_ffn_d1_gnn_r16_6a6ccc'

def setup_inputs(seed: int=0):
    np.random.seed(seed)
    _w = jnp.asarray

    def _rec_inputs():
        import jax
        import jax.numpy as jnp
        _gk = jax.random.key(seed)
        x = -0.000364 + 1 * jax.random.normal(jax.random.fold_in(_gk, 1), (3125, 768), jnp.float32)
        src = jax.random.randint(jax.random.fold_in(_gk, 2), (50000,), 0, 3125, jnp.int32)
        dst = jax.random.randint(jax.random.fold_in(_gk, 3), (50000,), 0, 3125, jnp.int32)
        _o = jnp.argsort(dst, stable=True)
        src = src[_o]
        dst = dst[_o]
        return (x, src, dst)
    x, src, dst = _rec_inputs()

    def _L0_gnn_setup():
        import jax, jax.numpy as jnp
        import numpy as np
        N_NODES = 1250
        N_EDGES = 6250
        D_IN = 768
        NEG_SLOPE = 0.2

        def _gat_layer(x, W, attn_l, attn_r, bias, src, dst, num_heads, head_dim, use_elu):
            N = x.shape[0]
            z = (x @ W).reshape(N, num_heads, head_dim)
            el = jnp.sum(z * attn_l, axis=-1)
            er = jnp.sum(z * attn_r, axis=-1)
            e = jax.nn.leaky_relu(el[src] + er[dst], NEG_SLOPE)
            m = jax.ops.segment_max(e, dst, num_segments=N)
            ex = jnp.exp(e - m[dst])
            denom = jax.ops.segment_sum(ex, dst, num_segments=N)
            alpha = ex / denom[dst]
            msg = alpha[:, :, None] * z[src]
            out = jax.ops.segment_sum(msg, dst, num_segments=N)
            out = out + z
            out = out + bias.reshape(1, num_heads, head_dim)
            if use_elu:
                out = jax.nn.elu(out)
            return out.reshape(N, num_heads * head_dim)
        key = jax.random.key(seed)
        ks = jax.random.split(key, 16)
        node_features = jax.random.normal(ks[0], (N_NODES, D_IN), dtype=jnp.float32)
        src = jax.random.randint(ks[1], (N_EDGES,), 0, N_NODES)
        dst = jax.random.randint(ks[2], (N_EDGES,), 0, N_NODES)
        s = 1.0 / np.sqrt(D_IN)
        inp = {'node_features': node_features, 'src': src, 'dst': dst}
        heads = [(12, 64), (12, 64), (1, 768)]
        for i, (H, D) in enumerate(heads):
            inp[f'W{i}'] = jax.random.normal(ks[3 + 4 * i], (D_IN, H * D), dtype=jnp.float32) * s
            inp[f'al{i}'] = jax.random.normal(ks[4 + 4 * i], (H, D), dtype=jnp.float32) * s
            inp[f'ar{i}'] = jax.random.normal(ks[5 + 4 * i], (H, D), dtype=jnp.float32) * s
            inp[f'b{i}'] = jnp.zeros((H * D,), dtype=jnp.float32)
        return inp
    _L0_gnn_all = _L0_gnn_setup()
    _L0_gnn_in = {k: v for k, v in _L0_gnn_all.items() if k in ('W0', 'al0', 'ar0', 'b0', 'W1', 'al1', 'ar1', 'b1', 'W2', 'al2', 'ar2', 'b2')}
    del _L0_gnn_all

    def _L0_ffn_setup():
        import jax, jax.numpy as jnp
        import numpy as np
        B, S, H, F, E, TOP_K = (4, 128, 768, 192, 8, 2)
        key = jax.random.key(seed)
        ks = jax.random.split(key, 6)
        x = jax.random.normal(ks[0], (B, S, H), dtype=jnp.float32)
        Wr = jax.random.normal(ks[1], (E, H), dtype=jnp.float32) * 0.02
        Wi = jax.random.normal(ks[2], (E, F, H), dtype=jnp.float32) * 0.02
        bi = jnp.zeros((E, F), dtype=jnp.float32)
        Wo = jax.random.normal(ks[3], (E, H, F), dtype=jnp.float32) * 0.02
        bo = jnp.zeros((E, H), dtype=jnp.float32)
        return {'x': x, 'Wr': Wr, 'Wi': Wi, 'bi': bi, 'Wo': Wo, 'bo': bo}
    _L0_ffn_all = _L0_ffn_setup()
    _L0_ffn_in = {k: v for k, v in _L0_ffn_all.items() if k in ('Wr', 'Wi', 'bi', 'Wo', 'bo')}
    del _L0_ffn_all
    return {'x': x, 'src': src, 'dst': dst, 'L0_gnn_W0': _L0_gnn_in['W0'], 'L0_gnn_al0': _L0_gnn_in['al0'], 'L0_gnn_ar0': _L0_gnn_in['ar0'], 'L0_gnn_b0': _L0_gnn_in['b0'], 'L0_gnn_W1': _L0_gnn_in['W1'], 'L0_gnn_al1': _L0_gnn_in['al1'], 'L0_gnn_ar1': _L0_gnn_in['ar1'], 'L0_gnn_b1': _L0_gnn_in['b1'], 'L0_gnn_W2': _L0_gnn_in['W2'], 'L0_gnn_al2': _L0_gnn_in['al2'], 'L0_gnn_ar2': _L0_gnn_in['ar2'], 'L0_gnn_b2': _L0_gnn_in['b2'], 'L0_ffn_Wr': _L0_ffn_in['Wr'], 'L0_ffn_Wi': _L0_ffn_in['Wi'], 'L0_ffn_bi': _L0_ffn_in['bi'], 'L0_ffn_Wo': _L0_ffn_in['Wo'], 'L0_ffn_bo': _L0_ffn_in['bo']}

def reference(x, src, dst, L0_gnn_W0, L0_gnn_al0, L0_gnn_ar0, L0_gnn_b0, L0_gnn_W1, L0_gnn_al1, L0_gnn_ar1, L0_gnn_b1, L0_gnn_W2, L0_gnn_al2, L0_gnn_ar2, L0_gnn_b2, L0_ffn_Wr, L0_ffn_Wi, L0_ffn_bi, L0_ffn_Wo, L0_ffn_bo):
    import jax
    import jax.numpy as jnp

    def _L0_gnn_ref(node_features, W0, al0, ar0, b0, W1, al1, ar1, b1, W2, al2, ar2, b2, src, dst):
        import jax, jax.numpy as jnp
        import numpy as np
        N_NODES = 1250
        N_EDGES = 6250
        D_IN = 768
        NEG_SLOPE = 0.2

        def _gat_layer(x, W, attn_l, attn_r, bias, src, dst, num_heads, head_dim, use_elu):
            N = x.shape[0]
            z = (x @ W).reshape(N, num_heads, head_dim)
            el = jnp.sum(z * attn_l, axis=-1)
            er = jnp.sum(z * attn_r, axis=-1)
            e = jax.nn.leaky_relu(el[src] + er[dst], NEG_SLOPE)
            m = jax.ops.segment_max(e, dst, num_segments=N)
            ex = jnp.exp(e - m[dst])
            denom = jax.ops.segment_sum(ex, dst, num_segments=N)
            alpha = ex / denom[dst]
            msg = alpha[:, :, None] * z[src]
            out = jax.ops.segment_sum(msg, dst, num_segments=N)
            out = out + z
            out = out + bias.reshape(1, num_heads, head_dim)
            if use_elu:
                out = jax.nn.elu(out)
            return out.reshape(N, num_heads * head_dim)
        x = _gat_layer(node_features, W0, al0, ar0, b0, src, dst, 12, 64, True)
        x = _gat_layer(x, W1, al1, ar1, b1, src, dst, 12, 64, True)
        x = _gat_layer(x, W2, al2, ar2, b2, src, dst, 1, 768, False)
        return x

    def _L0_ffn_ref(x, Wr, Wi, bi, Wo, bo):
        import jax, jax.numpy as jnp
        import numpy as np
        B, S, H, F, E, TOP_K = (4, 128, 768, 192, 8, 2)
        xf = x.reshape(-1, x.shape[-1])
        router_logits = jnp.einsum('th,eh->te', xf, Wr)
        topk_vals, topk_idx = jax.lax.top_k(router_logits, TOP_K)
        routing_weights = jax.nn.softmax(topk_vals, axis=-1)
        h = jnp.einsum('th,efh->etf', xf, Wi) + bi[:, None, :]
        h = jax.nn.gelu(h, approximate=False)
        expert_out = jnp.einsum('etf,ehf->eth', h, Wo) + bo[:, None, :]
        expert_out = jnp.transpose(expert_out, (1, 0, 2))
        gathered = jnp.take_along_axis(expert_out, topk_idx[:, :, None], axis=1)
        out = jnp.einsum('tk,tkh->th', routing_weights, gathered)
        return out.reshape(x.shape)
    x = x + _L0_gnn_ref(_layernorm(x, axis=-1), L0_gnn_W0, L0_gnn_al0, L0_gnn_ar0, L0_gnn_b0, L0_gnn_W1, L0_gnn_al1, L0_gnn_ar1, L0_gnn_b1, L0_gnn_W2, L0_gnn_al2, L0_gnn_ar2, L0_gnn_b2, src, dst)
    x = x + _L0_ffn_ref(_layernorm(x, axis=-1)[None], L0_ffn_Wr, L0_ffn_Wi, L0_ffn_bi, L0_ffn_Wo, L0_ffn_bo)[0]
    return x

_drawn_inputs = setup_inputs


def setup_inputs(seed=0):
    import zlib

    import numpy as np

    out = dict(_drawn_inputs(seed))
    spreads = {'L0_gnn_b0': (0.0, 0.1),
     'L0_gnn_b1': (0.0, 0.1),
     'L0_gnn_b2': (0.0, 0.1),
     'L0_ffn_bi': (0.0, 0.8),
     'L0_ffn_bo': (0.0, 0.1)}
    factors = {'L0_gnn_ar0': 5.005, 'L0_gnn_ar1': 6.214}
    for name, (base, spread) in spreads.items():
        noise = np.random.default_rng([zlib.crc32(name.encode()), seed]).standard_normal(out[name].shape)
        drawn = base * np.exp(spread * noise) if base else spread * noise
        out[name] = jnp.asarray(drawn.astype(out[name].dtype))
    for name, factor in factors.items():
        out[name] = (out[name] * factor).astype(out[name].dtype)
    return out
```

```python
from contextlib import ExitStack

import concourse.bass as bass
from concourse import mybir

F32 = mybir.dt.float32
BF16 = mybir.dt.bfloat16
I32 = mybir.dt.int32
U32 = mybir.dt.uint32
ALU = mybir.AluOpType
ACT = mybir.ActivationFunctionType
AX_X = mybir.AxisListType.X

P = 128
N, D = 3125, 768
NE = 50000
NB = -(-N // P)
NPAD = NB * P
LAST = N - (NB - 1) * P
KC = D // P
ET = -(-NE // P)
HEADS = (12, 12, 1)
HMAX = max(HEADS)
G = 5
NBUF = 3
U = G * NBUF
V = -(-(ET + NB - 1) // U) * U
NG = V // G
NI = NG // NBUF
ROW = D + HMAX
HALF = D // 2
EX, FF = 8, 192
F = EX * FF
FC = F // P
NO_NODE = -1.0
SLOPE = 0.2
EPS = 1e-5


class Chain:

    def __init__(self, eng, sem):
        self.eng, self.sem, self.base, self.turns = eng, sem, 0, 0

    def link(self, instruction):
        instruction.then_inc(self.sem, 1)
        self.base += 1
        self.eng.wait_ge(self.sem, self.base + self.turns)

    def enter(self, turn, per):
        self.start, self.per, self.turns = self.base, per, turn * per

    def leave(self, trips):
        assert self.base - self.start == self.per, (self.base - self.start, self.per)
        self.turns, self.base = 0, self.start + trips * self.per


class Block:

    def __init__(self, c, i=None):
        self.q = c % 2
        self.n = c if i is None else i * 2 + c
        self.turn = c // 2 if i is None else i + c // 2
        self.reuse = i is not None or c >= 2
        self.rows = LAST if i is None and c == NB - 1 else P
        self.fixed = i is None

    def row0(self):
        return self.n * P


def gnn_ffn(nc, x, src, dst, gnn, ffn, out):
    with ExitStack() as ctx:
        def sb(name, shape, dt=F32):
            return ctx.enter_context(nc.sbuf_tensor(name, shape, dt))

        def sem(name):
            return ctx.enter_context(nc.semaphore(name))

        edges = nc.dram_tensor("edges", (ET, 2 * P), I32, kind="Internal").ap()
        table = [nc.dram_tensor(f"table{l}", (NPAD, D + h), F32, kind="Internal").ap() for l, h in enumerate(HEADS)]
        mixed = [nc.dram_tensor(f"mixed{l}", (NPAD, D), F32, kind="Internal").ap() for l in range(3)]

        PS = ctx.enter_context(nc.psum_tensor("PS", [P, 8, 512], F32))
        arena = sb("arena", [P, U * ROW])
        W = sb("W", [P, 3, KC, D + 2 * HMAX])
        WoT = sb("WoT", [P, FC, D])
        WrT = sb("WrT", [P, KC * EX])
        bi_col = sb("bi_col", [P, FC])
        bo_sb = sb("bo_sb", [EX, D])
        expert_rows = sb("expert_rows", [FC, D + P])
        bias = sb("bias", [P, D])
        WiT = W[:, :, :, :].rearrange("p l k n -> p (l k n)")[:, 0:KC * F].rearrange("p (k f) -> p k f", k=KC)
        expert_of = sb("expert_of", [EX, F])
        ident = sb("ident", [P, P])
        ones = sb("ones", [P, P])
        zeros = sb("zeros", [P, D + 2 * HMAX])
        zeros_h = sb("zeros_h", [P, 512], BF16)
        iota_row = sb("iota_row", [P, P])
        iota_i = sb("iota_i", [P, V], I32)
        eps = sb("eps", [P, 2])
        src_k = sb("src_k", [P, V], I32)
        dst_k = sb("dst_k", [P, V])
        b_k = sb("b_k", [1, V + 1], I32)
        b_g = sb("b_g", [1, NG, 12], I32)
        ends = sb("ends", [1, NB], I32)
        erm = sb("erm", [P, NB, 2 * HMAX])
        ert = sb("ert", [P, NB, HMAX])
        gm = sb("gm", [P, HMAX])
        gmb = sb("gmb", [P, 2, HMAX])
        S = sb("S", [P, NBUF, G, P])
        ST = sb("ST", [P, NBUF, G, P])
        wt = sb("wt", [P, NBUF, G, HMAX])
        wu = sb("wu", [P, NBUF, G, HMAX])
        stage = sb("stage", [P, U], I32)
        sums = sb("sums", [P, 2, D])
        rec = sb("rec", [P, 2, HMAX])
        stats = sb("stats", [P, 2, 16])
        gate = sb("gate", [P, 96])
        gate_i = sb("gate_i", [P, 8], U32)
        gT = sb("gT", [EX, 2, P])

        def rows_buf(j, q, width=D):
            return arena[:, (2 * j + q) * D:(2 * j + q) * D + width]

        def zr(q, width):
            return arena[:, 12 * D + q * (D + 2 * HMAX):12 * D + q * (D + 2 * HMAX) + width]

        in0, in1, in2, xr, xT, x2 = (lambda q, j=j: rows_buf(j, q) for j in range(6))
        hid = ST[:, :, :, :].rearrange("p a b c -> p (a b c)")
        hg = S[:, :, :, :].rearrange("p a b c -> p (a b c)")

        s_const = sem("s_const"); s_cload = sem("s_cload"); s_pad = sem("s_pad"); s_dst = sem("s_dst")
        s_prep = sem("s_prep"); s_cnt = sem("s_cnt"); s_tk = sem("s_tk"); s_tki = sem("s_tki")
        s_rows_k = sem("s_rows_k"); s_rows_f = sem("s_rows_f"); s_turned = sem("s_turned"); s_tables = sem("s_tables")
        s_w = [sem(f"s_w{l}") for l in range(3)]; s_waug = sem("s_waug"); s_al = sem("s_al"); s_al_used = sem("s_al_used")
        s_wld = [sem("s_wld0"), sem("s_wld1")]; s_wol = [sem("s_wol0"), sem("s_wol1")]; s_wT = sem("s_wT"); s_wcp = sem("s_wcp"); s_bias = sem("s_bias")
        s_in = [sem("s_in0"), sem("s_in1")]
        s_in_used = sem("s_in_used"); s_stat = sem("s_stat"); s_std = sem("s_std")
        s_rows = sem("s_rows"); s_xTp = sem("s_xTp"); s_xT = sem("s_xT"); s_zp = sem("s_zp"); s_zr = sem("s_zr")
        s_tab = sem("s_tab"); s_stored = [sem("s_stored0"), sem("s_stored1")]
        s_gmT = sem("s_gmT"); s_diag = sem("s_diag"); s_gmB = sem("s_gmB"); s_erm = sem("s_erm")
        s_staged = sem("s_staged"); s_tick = sem("s_tick")
        s_z = [sem(f"s_z{j}") for j in range(U)]
        s_S = sem("s_S"); s_STp = sem("s_STp"); s_ST = sem("s_ST"); s_er = sem("s_er"); s_pre = sem("s_pre")
        s_exp = sem("s_exp"); s_msg = sem("s_msg"); s_agg = sem("s_agg"); s_acc_free = sem("s_acc_free")
        s_sums = sem("s_sums"); s_sums_free = sem("s_sums_free"); s_sums_st = sem("s_sums_st")
        s_lg = sem("s_lg"); s_d = sem("s_d"); s_e = sem("s_e"); s_g = sem("s_g"); s_gTp = sem("s_gTp"); s_gT = sem("s_gT")
        s_hp = sem("s_hp"); s_gelu = sem("s_gelu"); s_gx = sem("s_gx"); s_hg = sem("s_hg"); s_op = sem("s_op")
        s_or = sem("s_or"); s_or_st = [sem("s_or_st0"), sem("s_or_st1")]
        s_dve = sem("s_dve"); s_acts = sem("s_acts"); s_pool = sem("s_pool"); s_close = sem("s_close"); s_tick_dve = sem("s_tick_dve")

        AHEAD = U

        def sweep_nodes(eng, stages, chain=None, per=0):
            def steps(i, ts):
                for t in ts:
                    for stage, lead in stages:
                        if i is not None or 0 <= t + lead < NB:
                            stage(Block(t + lead, i))

            steps(None, range(-max(lead for _, lead in stages), 2))
            trips = (NB - 5) // 2
            with eng.Fori(1, 1 + trips) as i:
                if chain:
                    chain.enter(i - 1, per)
                steps(i, (0, 1))
            if chain:
                chain.leave(trips)
            steps(None, range(NB - 3, NB))

        def free_again(eng, b, sem, l):
            if b.reuse:
                eng.wait_ge(sem, b.n + (NB * l - 1))

        def z_width(l):
            return D + 2 * HEADS[l]

        def flat_banks(b):
            return PS[:, b:b + 2, :].rearrange("p b n -> p (b n)")

        def edge_heads(l, jj):
            w = D + HEADS[l]
            return arena[:, 0:U * w].rearrange("p (u n) -> p u n", u=U)[:, jj * G:(jj + 1) * G, D:w]

        def bk_f():
            return arena[:, 9700:9700 + V]

        def ert_flat(l):
            return ert[:, :, :].rearrange("p b h -> p (b h)")[:, 0:NB * HEADS[l]]

        def wcount():
            return arena[0:125, 400 * 24:401 * 24]

        def tk_row():
            return arena[0:1, U * ROW - V:U * ROW]

        def rows_f():
            return arena[:, 4 * 2 * P:8 * 2 * P]

        def wo_rows(h):
            return arena[:, (4 + 2 * (h % 2)) * D:(6 + 2 * (h % 2)) * D]

        def wr_rows():
            return expert_rows[0:EX, 0:D]

        def bi_rows():
            return expert_rows[0:FC, D:D + P]

        def erm_flat(l):
            return erm[:, :, :].rearrange("p b h -> p (b h)")[:, 0:NB * 2 * HEADS[l]]

        block = ctx.enter_context(nc.Block())

        @block.sync
        def _(sp):
            flat_S = S[:, :, :, :].rearrange("p a b c -> p (a b c)")
            sp.dma_start(flat_S[0:125, 0:400].bitcast(I32), dst.rearrange("(p e) -> p e", p=125)).then_inc(s_dst, 16)
            full = NE // P * P
            sp.dma_start(edges[0:ET - 1, 0:P], src[0:full].rearrange("(t e) -> t e", e=P)).then_inc(s_pad, 16)
            sp.dma_start(edges[0:ET - 1, P:2 * P], dst[0:full].rearrange("(t e) -> t e", e=P)).then_inc(s_pad, 16)
            sp.dma_start(edges[ET - 1:ET, 0:NE - full], src[full:NE].rearrange("(t e) -> t e", t=1)).then_inc(s_pad, 16)
            sp.dma_start(edges[ET - 1:ET, P:P + NE - full], dst[full:NE].rearrange("(t e) -> t e", t=1)).then_inc(s_pad, 16)
            sp.wait_ge(s_const, 3)
            pad = P - (NE - full)
            sp.dma_start(edges[ET - 1:ET, NE - full:P], src_k[0:1, 0:pad]).then_inc(s_pad, 16)
            sp.dma_start(edges[ET - 1:ET, P + NE - full:2 * P], src_k[0:1, P:P + pad]).then_inc(s_pad, 16)

            def load(l):
                last = l == 3

                def begin(b):
                    free_again(sp, b, s_in_used, l)
                    ins = []
                    if l == 0 or last:
                        to = in2 if last else in0
                        ins.append((to(b.q)[0:b.rows], x[bass.ds(b.row0(), b.rows), :]))
                    if l:
                        ins.append((in0(b.q), mixed[l - 1][bass.ds(b.row0(), P), :]))
                        ins.append((in1(b.q), table[l - 1][bass.ds(b.row0(), P), 0:D]))
                    for o, i in ins:
                        sp.dma_start(o, i).then_inc(s_in[b.q], 16)
                return begin

            for l in range(4):
                if l == 0:
                    sp.wait_ge(s_waug, 3)
                if l:
                    sp.wait_ge(s_sums_st, 16 * NB * l)
                    sp.dma_start(bias[:, :], gnn[3 * 0 + l - 1]["b"].partition_broadcast(P)).then_inc(s_bias, 16)
                sweep_nodes(sp, [(load(l), 0)])
                if l == 2:
                    sp.wait_ge(s_stored[0], 16 * (NB // 2 + 1) * 3)
                    sp.wait_ge(s_stored[1], 16 * (NB // 2) * 3)
                    for u in range(12):
                        if u >= 2:
                            sp.wait_ge(s_wT, u - 1)
                        sp.dma_start(rows_buf(u % 2, 0), ffn["Wi"].rearrange("e f d -> (e f) d")[u * P:(u + 1) * P, :]).then_inc(s_wld[u % 2], 16)
                    for h in range(KC):
                        if h >= 2:
                            sp.wait_ge(s_wT, 12 + 2 * (h - 1))
                        sp.dma_start(wo_rows(h).rearrange("p (e f) -> p e f", e=EX),
                                     ffn["Wo"][:, h * P:(h + 1) * P, :].rearrange("e p f -> p e f")).then_inc(s_wol[h % 2], 16)
                if l < 3:
                    def sums_out(n, q):
                        sp.wait_ge(s_sums, n + (NB * l + 1))
                        sp.dma_start(mixed[l][bass.ds(n * P, P), :],
                                     sums[:, q, :]).then_inc(s_sums_st, 16)
                        sp.wait_ge(s_sums_st, 16 * n + 16 * (NB * l + 1))
                        sp.sem_inc(s_sums_free, 1)
                    with sp.Fori(0, NB // 2) as i:
                        for c in (0, 1):
                            sums_out(i * 2 + c, (NB * l + c) % 2)
                    sums_out(NB - 1, (NB * l + NB - 1) % 2)

        @block.gpsimd
        def _(pool):
            pc = Chain(pool, s_pool)
            pc.link(nc.gpsimd.memset(src_k[0:1, 0:P], 0))
            nc.gpsimd.memset(src_k[0:1, P:2 * P], int(NO_NODE)).then_inc(s_const, 3)
            pc.link(nc.gpsimd.memset(ident[:, :], 0.0))
            nc.gpsimd.affine_select(out=ident[:, :], in_=ident[:, :], compare_op=ALU.not_equal, fill=1.0, base=0,
                                    pattern=[[-1, P]], channel_multiplier=1).then_inc(s_const, 1)
            nc.gpsimd.memset(ones[:, :], 1.0).then_inc(s_const, 1)
            nc.gpsimd.memset(zeros[:, :], 0.0).then_inc(s_const, 1)
            nc.gpsimd.memset(zeros_h[:, :], 0.0).then_inc(s_const, 1)
            nc.gpsimd.memset(eps[:, 0:1], EPS).then_inc(s_const, 1)
            nc.gpsimd.memset(eps[:, 1:2], -1.0).then_inc(s_const, 1)
            nc.gpsimd.iota(iota_i[:, :], pattern=[[1, V]], base=0, channel_multiplier=0).then_inc(s_const, 1)
            pc.link(nc.gpsimd.memset(expert_of[:, :], 1.0))
            pc.link(nc.gpsimd.affine_select(out=expert_of[:, :], in_=expert_of[:, :], compare_op=ALU.is_ge, fill=0.0,
                                            base=0, pattern=[[1, F]], channel_multiplier=-FF))
            nc.gpsimd.affine_select(out=expert_of[:, :], in_=expert_of[:, :], compare_op=ALU.is_ge, fill=0.0,
                                    base=FF - 1, pattern=[[-1, F]], channel_multiplier=FF).then_inc(s_const, 1)

            ek = arena[:, 0:4 * 2 * P].bitcast(I32)
            tki = gate[:, 0:4].bitcast(U32)
            pool.wait_ge(s_pad, 16 * 6)
            pool.wait_ge(s_tki, 2)
            pool.sem_inc(s_tick)
            for c in range(4):
                n = min(P, V - c * P)
                nc.gpsimd.indirect_dma_start(ek[0:n, c * 2 * P:(c + 1) * 2 * P], None, edges[:, :],
                                             bass.IndirectOffsetOnAxis(tki[0:n, c:c + 1], 0)).then_inc(s_rows_k, 16)

            def store(l):
                def run(b):
                    pool.wait_ge(s_zr, b.n + (NB * l + 1))
                    pool.sem_inc(s_tick)
                    nc.gpsimd.dma_start(table[l][bass.ds(b.row0(), P), :],
                                        zr(b.q, D + HEADS[l])).then_inc(s_stored[b.q], 16)
                return run

            def store_out(b):
                pool.wait_ge(s_or, b.n + 1)
                pool.sem_inc(s_tick)
                nc.gpsimd.dma_start(out[bass.ds(b.row0(), b.rows), :], zr(b.q, D)[0:b.rows]).then_inc(s_or_st[b.q], 16)

            for l in range(3):
                sweep_nodes(pool, [(store(l), 0)])
                pool.wait_ge(s_stored[0], 16 * (NB // 2 + 1) * (l + 1))
                pool.wait_ge(s_stored[1], 16 * (NB // 2) * (l + 1))
                pool.wait_ge(s_tab, NB * (l + 1))
                pool.wait_ge(s_tables, 1)
                if l == 2:
                    pool.wait_ge(s_wT, 24)
                pool.sem_inc(s_tick)
                with pool.Fori(0, NI) as i:
                    for jj in range(NBUF):
                        pool.wait_ge(s_agg, U * i + (G * (jj + 1) + V * l))
                        pool.sem_inc(s_tick)
                        nc.gpsimd.tensor_copy(stage[:, jj * G:(jj + 1) * G],
                                              src_k[:, bass.ds(i * U + jj * G, G)]).then_inc(s_staged, 1)
                        pool.wait_ge(s_staged, NBUF * i + (jj + 1 + NG * l))
                        pool.sem_inc(s_tick)
                        for j in range(jj * G, (jj + 1) * G):
                            w = D + HEADS[l]
                            nc.gpsimd.indirect_dma_start(
                                arena[:, j * w:(j + 1) * w], None, table[l][:, :],
                                bass.IndirectOffsetOnAxis(stage[:, j:j + 1].bitcast(U32), 0)).then_inc(s_z[j], 16)

            sweep_nodes(pool, [(store_out, 0)])
            pool.wait_ge(s_or_st[0], 16 * (NB // 2 + 1))
            pool.wait_ge(s_or_st[1], 16 * (NB // 2))

        @block.scalar
        def _(act):
            ac = Chain(act, s_acts)
            for l in range(3):
                act.dma_start(W[:, l, :, 0:D], gnn[l]["W"].rearrange("(k p) n -> p k n", p=P)).then_inc(s_w[l], 16)
            act.dma_start(bo_sb[:, :], ffn["bo"]).then_inc(s_cload, 16)
            act.dma_start(expert_rows[0:EX, 0:D], ffn["Wr"]).then_inc(s_cload, 16)
            act.dma_start(expert_rows[:, D:D + P], ffn["bi"].rearrange("e f -> (e f)").rearrange("(c p) -> c p", p=P)).then_inc(s_cload, 16)
            albc = [arena[:, (8 + j) * D:(9 + j) * D] for j in range(2)]
            for l in range(3):
                if l:
                    act.wait_ge(s_al_used, l)
                else:
                    act.wait_ge(s_prep, 3)
                for j, name in enumerate(("al", "ar")):
                    act.dma_start(albc[j], gnn[l][name].rearrange("h d -> (h d)").partition_broadcast(P)).then_inc(s_al, 16)

            def make_xT(l, banks):
                def xt(b):
                    act.wait_ge(s_xTp, b.n + (NB * l + 1))
                    if l < 3:
                        free_again(act, b, s_zp, l)
                    else:
                        free_again(act, b, s_op, 0)
                    nc.scalar.activation(xT(b.q), banks(b.q)[:, 0:D], ACT.Copy).then_inc(s_xT, 1)
                return xt

            def std(b, k):
                act.wait_ge(s_stat, b.n + (NB * k + 1))
                nc.scalar.activation(stats[:, b.q, 14:15], stats[:, b.q, 13:14], ACT.Sqrt,
                                     bias=eps[:, 0:1]).then_inc(s_std, 1)

            def node_sweep(l):
                xt = make_xT(l, lambda q: flat_banks(2 * q))

                def finish_rows(b):
                    if l == 0:
                        std(b, 0)
                    else:
                        act.wait_ge(s_stat, b.n + (NB * l + 1))
                        ac.link(nc.scalar.activation(in1(b.q), in1(b.q), ACT.Exp))
                        nc.scalar.activation(in1(b.q), in1(b.q), ACT.Identity, bias=eps[:, 1:2]).then_inc(s_std, 1)

                def copy_z(b):
                    act.wait_ge(s_zp, b.n + (NB * l + 1))
                    if b.reuse:
                        act.wait_ge(s_stored[b.q], 16 * b.turn + 16 * (NB // 2 + (1 - b.q)) * l)
                    free_again(act, b, s_tab, l)
                    nc.scalar.activation(zr(b.q, z_width(l)), flat_banks(4 + 2 * b.q)[:, 0:z_width(l)],
                                         ACT.Copy).then_inc(s_zr, 1)

                sweep_nodes(act, [(finish_rows, 2), (xt, 1), (copy_z, 0)], ac if l else None, 2)

            def ffn_weights():
                for u in range(24):
                    if u < 12:
                        at, frm = rows_buf(u % 2, 0), ffn["Wi"].rearrange("e f d -> (e f) d")[u * P:(u + 1) * P, :]
                        to = WiT[:, :, u * P:(u + 1) * P]
                    else:
                        h, half = divmod(u - 12, 2)
                        to = WoT[:, half * 6:half * 6 + 6, h * P:(h + 1) * P]
                    act.wait_ge(s_wT, u + 1)
                    nc.scalar.activation(to, flat_banks(2 * (u % 2))[:, 0:D].rearrange("p (k f) -> p k f", k=6),
                                         ACT.Copy).then_inc(s_wcp, 1)

            def edge_sweep(l):
                H = HEADS[l]

                def copy_ST(g, jj):
                    act.wait_ge(s_STp, g + (NG * l + 1))
                    nc.scalar.activation(ST[:, jj, :, :].rearrange("p g e -> p (g e)"), flat_banks(4)[:, 0:G * P],
                                         ACT.Copy).then_inc(s_ST, 1)

                def body(i, last):
                    for jj in range(NBUF):
                        g = NBUF * i + jj
                        act.wait_ge(s_pre, g + (NG * l + 1))
                        nc.scalar.activation(edge_heads(l, jj), wt[:, jj, :, 0:H], ACT.Exp).then_inc(s_exp, 1)
                        if not (last and jj == NBUF - 1):
                            copy_ST(g + 1, (jj + 1) % NBUF)

                copy_ST(0, 0)
                with act.Fori(0, NI - 1) as i:
                    body(i, False)
                body(NI - 1, True)

            for l in range(3):
                node_sweep(l)
                if l == 2:
                    ffn_weights()
                edge_sweep(l)

            xt = make_xT(3, lambda q: flat_banks(0))

            def hidden(b):
                for grp in range(3):
                    m = 3 * b.n + grp
                    act.wait_ge(s_hp, m + 1)
                    if b.reuse or b.n or grp >= 2:
                        act.wait_ge(s_hg, m - 1)
                    half = (b.q + grp) % 2
                    for c in range(4):
                        o = nc.scalar.activation(hid[:, half * 512 + c * P:half * 512 + (c + 1) * P],
                                                 PS[:, 2 + half, c * P:(c + 1) * P], ACT.Gelu,
                                                 bias=bi_col[:, 4 * grp + c:4 * grp + c + 1])
                    o.then_inc(s_gelu, 1)
                    if grp == 0:
                        act.wait_ge(s_d, b.n + 1)
                        nc.scalar.activation(gate[:, 1:2], gate[:, 0:1], ACT.Exp).then_inc(s_e, 1)
                        act.wait_ge(s_gTp, b.n + 1)
                        nc.scalar.activation(gT[:, b.q, :], PS[0:EX, 7, P:2 * P], ACT.Copy).then_inc(s_gT, 1)

            sweep_nodes(act, [(hidden, 0), (lambda b: std(b, 3), 1), (xt, 1)])

        @block.tensor
        def _(pe):
            pe.sem_inc(s_agg, AHEAD)
            pe.sem_inc(s_acc_free, 2)
            pe.sem_inc(s_sums_free, 2)
            pe.wait_ge(s_const, 11)
            pe.wait_ge(s_prep, 1)
            nc.tensor.matmul(PS[:, 0, 0:NB - 1], ones[0:125, :], wcount(), start=True, stop=True).then_inc(s_cnt, 1)
            pe.wait_ge(s_prep, 2)
            for c in range(4):
                n = min(P, V - c * P)
                last = nc.tensor.matmul(PS[0:n, 1, c:c + 1], tk_row()[:, c * P:c * P + n], ones[0:1, 0:1],
                                        start=True, stop=True)
            last.then_inc(s_tk, 1)
            pe.wait_ge(s_rows_f, 1)
            for j in range(2):
                for c in range(4):
                    n = min(P, V - c * P)
                    last = nc.tensor.transpose(PS[:, 2 + j, c * P:c * P + n],
                                               rows_f()[0:n, (2 * c + j) * P:(2 * c + j + 1) * P], ident[0:n, 0:n])
            last.then_inc(s_turned, 1)

            def turn_rows(l, banks):
                def turn(b):
                    pe.wait_ge(s_rows, b.n + (NB * l + 1))
                    if l < 3:
                        free_again(pe, b, s_xT, l)
                    elif b.reuse or b.n:
                        pe.wait_ge(s_xT, b.n + NB * l)
                    for k in range(KC):
                        o = nc.tensor.transpose(banks(b.q)[:, k * P:(k + 1) * P], xr(b.q)[:, k * P:(k + 1) * P],
                                                ident[:, :])
                    o.then_inc(s_xTp, 1)
                return turn

            def node_sweep(l):
                def product(b, ks):
                    for k in ks:
                        lhsT = xT(b.q)[:, k * P:(k + 1) * P]
                        nc.tensor.matmul(PS[:, 4 + 2 * b.q, :], lhsT, W[:, l, k, 0:512], start=(k == 0), stop=(k == KC - 1))
                        o = nc.tensor.matmul(PS[:, 5 + 2 * b.q, 0:z_width(l) - 512], lhsT, W[:, l, k, 512:z_width(l)],
                                             start=(k == 0), stop=(k == KC - 1))
                    return o

                def first_half(b):
                    pe.wait_ge(s_xT, b.n + (NB * l + 1))
                    free_again(pe, b, s_zr, l)
                    product(b, range(KC // 2))

                def second_half(b):
                    product(b, range(KC // 2, KC)).then_inc(s_zp, 1)

                pe.wait_ge(s_waug, l + 1)
                if l:
                    pe.wait_ge(s_acc_free, 2 + NB * l)
                sweep_nodes(pe, [(first_half, 0), (turn_rows(l, lambda q: flat_banks(2 * q)), 1), (second_half, 0)])
                H = HEADS[l]
                pe.wait_ge(s_zr, NB * (l + 1))
                pe.wait_ge(s_tab, NB * (l + 1))
                nc.tensor.transpose(PS[0:H, 7, 0:P], gm[:, 0:H], ident[:, :]).then_inc(s_gmT, 1)
                pe.wait_ge(s_diag, l + 1)
                nc.tensor.matmul(PS[:, 7, P:P + H], ones[0:H, :], gmb[0:H, 0, 0:H], start=True, stop=True).then_inc(s_gmB, 1)

            def ffn_weights():
                for u in range(24):
                    if u < 12:
                        frm = lambda k: rows_buf(u % 2, 0)[:, k * P:(k + 1) * P]
                        pe.wait_ge(s_wld[u % 2], 16 * (u // 2 + 1))
                    else:
                        h, half = divmod(u - 12, 2)
                        frm = lambda k: wo_rows(h)[:, (half * 6 + k) * P:(half * 6 + k + 1) * P]
                        if half == 0:
                            pe.wait_ge(s_wol[h % 2], 16 * (h // 2 + 1))
                    if u >= 2:
                        pe.wait_ge(s_wcp, u - 1)
                    for k in range(6):
                        o = nc.tensor.transpose(flat_banks(2 * (u % 2))[:, k * P:(k + 1) * P], frm(k), ident[:, :])
                    o.then_inc(s_wT, 1)

            def edge_sweep(l):
                H = HEADS[l]
                for bank in range(4):
                    nc.tensor.matmul(PS[:, bank, :], zeros_h[:, 0:P], zeros_h[:, :], start=True, stop=True)

                def turn_S(g, jj):
                    pe.wait_ge(s_S, g + (NG * l + 1))
                    for j in range(G):
                        o = nc.tensor.transpose(flat_banks(4)[:, j * P:(j + 1) * P], S[:, jj, j, :], ident[:, :])
                    o.then_inc(s_STp, 1)

                def blocks_of(g):
                    return nc.values_load_multi_w_load_instructions(
                        b_g[0:1, bass.ds(g, 1), 0:G].rearrange("o g j -> o (g j)"), engines=[mybir.EngineType.PE],
                        min_val=0, max_val=NB - 1)[1]

                def er_of_edges(g, jj, blocks):
                    pe.wait_ge(s_ST, g + (NG * l + 1))
                    for j, b in enumerate(blocks):
                        o = nc.tensor.matmul(PS[:, 6, (jj * G + j) * 2 * H:(jj * G + j + 1) * 2 * H], ST[:, jj, j, :],
                                             erm_flat(l)[:, bass.ds(b * (2 * H), 2 * H)], start=True, stop=True)
                    o.then_inc(s_er, 1)

                def add_up(g, jj, j, b):
                    k = g * G + j
                    w = D + H
                    slot = jj * G + j
                    odd = (b + l) % 2
                    pe.wait_ge(s_msg, k + (V * l + 1))
                    pe.wait_ge(s_acc_free, b + (NB * l + 1))
                    flat = PS[:, :, :].rearrange("p b n -> p (b n)")
                    nc.tensor.matmul(flat[:, bass.ds(odd * 1024, HALF)], S[:, jj, j, :], arena[:, slot * w:slot * w + HALF],
                                     start=False, stop=True, skip_group_check=True)
                    nc.tensor.matmul(flat[:, bass.ds(odd * 1024 + 512, HALF + H)], S[:, jj, j, :],
                                     arena[:, slot * w + HALF:(slot + 1) * w],
                                     start=False, stop=True, skip_group_check=True).then_inc(s_agg, 1)

                def body(i, last):
                    now, then = blocks_of(NBUF * i), blocks_of(NBUF * i + 1)
                    for jj in range(NBUF):
                        g = NBUF * i + jj
                        if not (last and jj == NBUF - 1):
                            er_of_edges(g + 1, (jj + 1) % NBUF, then)
                        after = None
                        for j in range(G):
                            if j == 1 and not (last and jj >= NBUF - 2):
                                after = blocks_of(g + 2)
                            if j == G - 1 and not (last and jj >= NBUF - 2):
                                turn_S(g + 2, (jj + 2) % NBUF)
                            add_up(g, jj, j, now[j])
                        now, then = then, after

                pe.wait_ge(s_erm, l + 1)
                turn_S(0, 0)
                er_of_edges(0, 0, blocks_of(0))
                turn_S(1, 1)
                with pe.Fori(0, NI - 1) as i:
                    body(i, False)
                body(NI - 1, True)

            for l in range(3):
                node_sweep(l)
                if l == 2:
                    ffn_weights()
                    pe.wait_ge(s_wcp, 24)
                edge_sweep(l)

            turn = turn_rows(3, lambda q: flat_banks(0))
            pe.wait_ge(s_acc_free, 2 + NB * 3)
            pe.wait_ge(s_cload, 16 * 3)
            for k in range(KC):
                nc.tensor.transpose(PS[:, 2, k * EX:(k + 1) * EX], wr_rows()[:, k * P:(k + 1) * P], ident[0:EX, 0:EX])
            nc.tensor.transpose(PS[:, 3, 0:FC], bi_rows(), ident[0:FC, 0:FC]).then_inc(s_wT, 1)
            pe.wait_ge(s_wcp, 26)

            def experts(b):
                pe.wait_ge(s_xT, b.n + (NB * 3 + 1))
                if b.reuse or b.n:
                    pe.wait_ge(s_g, b.n)
                for k in range(KC):
                    o = nc.tensor.matmul(PS[:, 7, 0:EX], xT(b.q)[:, k * P:(k + 1) * P], WrT[:, k * EX:(k + 1) * EX],
                                         start=(k == 0), stop=(k == KC - 1))
                o.then_inc(s_lg, 1)

                def up(grp):
                    m = 3 * b.n + grp
                    if b.reuse or b.n or grp >= 2:
                        pe.wait_ge(s_gelu, m - 1)
                    for c in range(4):
                        for k in range(KC):
                            f = (4 * grp + c) * P
                            o = nc.tensor.matmul(PS[:, 2 + (b.q + grp) % 2, c * P:(c + 1) * P], WiT[:, k, f:f + P],
                                                 xT(b.q)[:, k * P:(k + 1) * P], start=(k == 0), stop=(k == KC - 1))
                    o.then_inc(s_hp, 1)

                def spread(grp):
                    if b.reuse or b.n or grp:
                        pe.wait_ge(s_hg, 3 * b.n + grp)
                    for c in range(4):
                        f = (4 * grp + c) * P
                        o = nc.tensor.matmul(PS[:, 4, c * P:(c + 1) * P], expert_of[:, f:f + P], gT[:, b.q, :],
                                             start=True, stop=True)
                    o.then_inc(s_gx, 1)

                up(0)
                pe.wait_ge(s_g, b.n + 1)
                nc.tensor.transpose(PS[0:EX, 7, P:2 * P], gate[:, 32:32 + EX], ident[:, :]).then_inc(s_gTp, 1)
                up(1)
                pe.wait_ge(s_gT, b.n + 1)
                spread(0)
                up(2)
                spread(1)
                if b.reuse or b.n:
                    pe.wait_ge(s_or, b.n)
                down(b, 0)
                spread(2)
                down(b, 1)

            def down(b, grp):
                pe.wait_ge(s_hg, 3 * b.n + grp + 1)
                for c in range(4 * grp, 4 * grp + 4):
                    nc.tensor.matmul(PS[:, 5, :], hg[:, c * P:(c + 1) * P], WoT[:, c, 0:512], start=(c == 0), stop=False)
                    nc.tensor.matmul(PS[:, 6, 0:D - 512], hg[:, c * P:(c + 1) * P], WoT[:, c, 512:D],
                                     start=(c == 0), stop=False)

            def rest(b):
                down(b, 2)
                nc.tensor.matmul(PS[:, 5, :], gT[:, b.q, :], bo_sb[:, 0:512], start=False, stop=True)
                nc.tensor.matmul(PS[:, 6, 0:D - 512], gT[:, b.q, :], bo_sb[:, 512:D], start=False, stop=True).then_inc(s_op, 1)

            sweep_nodes(pe, [(experts, 0), (turn, 1), (rest, 0)])

        @block.vector
        def _(dve):
            dc = Chain(dve, s_dve)
            link = dc.link
            dve.wait_ge(s_const, 11)
            dst_f = arena[0:125, 0:400]
            link(nc.vector.tensor_copy(iota_row[:, :], iota_i[:, 0:P]))
            iota_f = arena[:, 10600:10600 + V]
            link(nc.vector.tensor_copy(iota_f, iota_i[:, :]))
            first = gate[:, 8:8 + NB - 1]
            link(nc.vector.tensor_scalar(first, iota_f[:, 0:NB - 1], float(P), float(P), ALU.mult, ALU.add))
            dve.wait_ge(s_dst, 16)
            dsti = S[:, :, :, :].rearrange("p a b c -> p (a b c)")[0:125, 0:400].bitcast(I32)
            dstf = S[:, :, :, :].rearrange("p a b c -> p (a b c)")[0:125, 400:800]
            link(nc.vector.tensor_copy(dstf, dsti))
            below = arena[0:125, 0:24 * 400].rearrange("p (b e) -> p b e", b=24)
            link(nc.vector.tensor_tensor(below, dstf.unsqueeze(1).broadcast_to([125, 24, 400]),
                                         first[0:125, :].unsqueeze(2).broadcast_to([125, 24, 400]), ALU.is_lt))
            nc.vector.tensor_reduce(wcount(), below, AX_X, ALU.add).then_inc(s_prep, 1)
            dve.wait_ge(s_cnt, 1)
            ti = wu[:, 0:2, :, :].rearrange("p a g h -> p (a g h)")[:, 0:NB - 1].bitcast(I32)
            link(nc.vector.tensor_copy(ti, PS[:, 0, 0:NB - 1]))
            link(nc.vector.tensor_scalar(ti, ti, 7, None, ALU.arith_shift_right))
            enter = gate[:, 8:8 + NB - 1]
            link(nc.vector.tensor_copy(enter, ti))
            link(nc.vector.tensor_scalar(enter, enter, float(ET - 1), None, ALU.min))
            link(nc.vector.scalar_tensor_tensor(out=enter, in0=iota_f[:, 0:NB - 1], scalar=1.0, in1=enter,
                                                op0=ALU.add, op1=ALU.add))
            for k0 in (0, V // 2):
                at = arena[:, 0:V // 2 * 24].rearrange("p (k b) -> p k b", b=24)
                link(nc.vector.tensor_tensor(at, iota_f[:, k0:k0 + V // 2].unsqueeze(2).broadcast_to([P, V // 2, 24]),
                                             enter.unsqueeze(1).broadcast_to([P, V // 2, 24]), ALU.is_ge))
                link(nc.vector.tensor_reduce(bk_f()[:, k0:k0 + V // 2], at, AX_X, ALU.add))
            link(nc.vector.tensor_tensor(tk_row(), iota_f[0:1, :], bk_f()[0:1, :], ALU.subtract))
            nc.vector.tensor_scalar(tk_row(), tk_row(), float(ET - 1), None, ALU.min).then_inc(s_prep, 1)
            link(nc.vector.tensor_copy(b_k[0:1, 0:V], bk_f()[0:1, :]))
            link(nc.vector.memset(b_k[0:1, V:V + 1], NB))
            starts = b_k[0:1, 0:V].rearrange("o (g j) -> o g j", j=G)
            link(nc.vector.tensor_copy(b_g[0:1, :, 0:G], starts))
            link(nc.vector.tensor_copy(b_g[0:1, :, 8:9], starts[:, :, 0:1]))
            link(nc.vector.tensor_copy(b_g[0:1, 0:NG - 1, 9:10], starts[:, 1:NG, 0:1]))
            link(nc.vector.memset(b_g[0:1, NG - 1:NG, 9:10], NB))
            link(nc.vector.tensor_copy(ends[0:1, 0:NB - 1], enter[0:1, :]))
            link(nc.vector.memset(ends[0:1, NB - 1:NB], V))
            dve.wait_ge(s_tk, 1)
            nc.vector.tensor_copy(gate[:, 0:3].bitcast(U32), PS[:, 1, 0:3]).then_inc(s_tki, 1)
            nc.vector.tensor_copy(gate[0:V - 3 * P, 3:4].bitcast(U32), PS[0:V - 3 * P, 1, 3:4]).then_inc(s_tki, 1)
            dve.wait_ge(s_rows_k, 16 * 4)
            nc.vector.tensor_copy(rows_f(), arena[:, 0:4 * 2 * P].bitcast(I32)).then_inc(s_rows_f, 1)
            dve.wait_ge(s_turned, 1)
            link(nc.vector.tensor_copy(src_k[:, :], PS[:, 2, 0:V]))
            link(nc.vector.scalar_tensor_tensor(out=dst_k[:, :], in0=bk_f(), scalar=-float(P), in1=PS[:, 3, 0:V],
                                                op0=ALU.mult, op1=ALU.add))
            nc.vector.memset(dst_k[:, ET + NB - 1:V], NO_NODE).then_inc(s_tables, 1)
            dve.wait_ge(s_tables, 1)
            nc.vector.tensor_copy(gate[:, 90:91], zeros[:, 0:1]).then_inc(s_prep, 1)

            for l in range(3):
                H = HEADS[l]
                dve.wait_ge(s_w[l], 16)
                dve.wait_ge(s_al, 32 * (l + 1))
                prod = arena[:, 7 * D:8 * D]
                for k in range(KC):
                    for j in range(2):
                        link(nc.vector.tensor_tensor(prod, W[:, l, k, 0:D], arena[:, (8 + j) * D:(9 + j) * D], ALU.mult))
                        link(nc.vector.tensor_reduce(W[:, l, k, D + j * H:D + (j + 1) * H],
                                                     prod.rearrange("p (h d) -> p h d", h=H), AX_X, ALU.add))
                nc.vector.tensor_copy(gate[:, 90:91], zeros[:, 0:1]).then_inc(s_al_used, 1)
            dve.wait_ge(s_al_used, 3)
            nc.vector.tensor_copy(gate[:, 91:92], zeros[:, 0:1]).then_inc(s_waug, 3)

            def in_ready(b, l):
                per = (1, 2, 2, 3)[l]
                uses = NB // 2 + 1 - b.q
                dve.wait_ge(s_in[b.q], 16 * per * b.turn + 16 * (per + uses * sum((1, 2, 2, 3)[:l])))

            def layernorm(b, rows, k, used):
                st = stats[:, b.q, :]
                nc.vector.bn_stats(st[:, 0:6], rows[:, 0:HALF])
                link(nc.vector.bn_stats(st[:, 6:12], rows[:, HALF:D]))
                dve.sem_inc(s_tick_dve)
                nc.vector.bn_aggr(st[:, 12:14], st[:, 0:12]).then_inc(s_stat, 1)
                dve.wait_ge(s_std, b.n + (NB * k + 1))
                link(nc.vector.reciprocal(st[:, 15:16], st[:, 14:15]))
                o = nc.vector.tensor_scalar(xr(b.q), rows, st[:, 12:13], st[:, 15:16], ALU.subtract, ALU.mult)
                return o

            def node_sweep(l):
                H = HEADS[l]

                def begin(b):
                    in_ready(b, l)
                    free_again(dve, b, s_xTp, l)
                    if l == 0:
                        link(layernorm(b, in0(b.q), 0, None))
                    else:
                        u, m = in0(b.q), in1(b.q)
                        link(nc.vector.tensor_tensor(u, u, m, ALU.add))
                        link(nc.vector.tensor_tensor(u, u, bias[:, :], ALU.add))
                        nc.vector.tensor_scalar(m, u, 0.0, None, ALU.min).then_inc(s_stat, 1)
                        dve.wait_ge(s_std, b.n + (NB * l + 1))
                        link(nc.vector.scalar_tensor_tensor(out=xr(b.q), in0=u, scalar=0.0, in1=m,
                                                            op0=ALU.max, op1=ALU.add))
                    dve.sem_inc(s_rows, 1)
                    dve.sem_inc(s_in_used, 1)

                def end(b):
                    dve.wait_ge(s_zr, b.n + (NB * l + 1))
                    nc.vector.tensor_copy(ert_flat(l)[:, bass.ds(b.n * H, H)], zr(b.q, D + 2 * H)[:, D + H:D + 2 * H])
                    link(nc.vector.tensor_tensor(gm[0:b.rows, 0:H], gm[0:b.rows, 0:H], zr(b.q, D + H)[0:b.rows, D:D + H],
                                                 ALU.max))
                    dve.sem_inc(s_tab, 1)

                link(nc.vector.memset(gm[:, :], -3.0e38))
                if l:
                    dve.wait_ge(s_bias, 16 * l)
                sweep_nodes(dve, [(begin, 2), (end, 0)], dc, 2 * (3 + 1))
                dve.wait_ge(s_gmT, l + 1)
                link(nc.vector.tensor_reduce(gmb[0:H, 1, 0:1], PS[0:H, 7, 0:P], AX_X, ALU.max))
                nc.vector.tensor_scalar(gmb[0:H, 0, 0:H], ident[0:H, 0:H], gmb[0:H, 1, 0:1], None,
                                        ALU.mult).then_inc(s_diag, 1)
                dve.wait_ge(s_gmB, l + 1)
                e3 = erm_flat(l).rearrange("p (b h) -> p b h", b=NB)
                ert3 = ert_flat(l).rearrange("p (b h) -> p b h", b=NB)
                link(nc.vector.tensor_copy(e3[:, :, 0:H], ert3))
                link(nc.vector.tensor_tensor(ert3, ert3, PS[:, 7, P:P + H].unsqueeze(1).broadcast_to([P, NB, H]), ALU.add))
                nc.vector.scalar_tensor_tensor(out=e3[:, :, H:2 * H], in0=ert3, scalar=SLOPE, in1=ert3,
                                               op0=ALU.mult, op1=ALU.max).then_inc(s_erm, 1)

            def edge_sweep(l):
                H = HEADS[l]
                w = D + H
                rows3 = arena[:, 0:U * w].rearrange("p (u n) -> p u n", u=U)

                def one_hots(g, jj):
                    dve.wait_ge(s_agg, G * g + (V * l + AHEAD - 2 * G))
                    to = dst_k[:, bass.ds(g * G, G)].unsqueeze(2).broadcast_to([P, G, P])
                    nc.vector.tensor_tensor(S[:, jj, :, :], iota_row[:, :].unsqueeze(1).broadcast_to([P, G, P]), to,
                                            ALU.is_equal).then_inc(s_S, 1)

                def exponents(g, i, jj):
                    dve.wait_ge(s_er, g + (NG * l + 1))
                    for j in range(jj * G, (jj + 1) * G):
                        dve.wait_ge(s_z[j], 16 * i + 16 * (NI * l + 1))
                    er = PS[:, 6, jj * G * 2 * H:(jj + 1) * G * 2 * H].rearrange("p (g h) -> p g h", g=G)
                    t, u = wt[:, jj, :, 0:H], wu[:, jj, :, 0:H]
                    link(nc.vector.tensor_tensor(u, edge_heads(l, jj), er[:, :, 0:H], ALU.add))
                    link(nc.vector.scalar_tensor_tensor(out=u, in0=u, scalar=SLOPE, in1=u, op0=ALU.mult, op1=ALU.max))
                    link(nc.vector.tensor_tensor(u, u, er[:, :, H:2 * H], ALU.subtract))
                    nc.vector.tensor_scalar(t, u, 0.0, None, ALU.min).then_inc(s_pre, 1)

                def weigh(g, jj):
                    dve.wait_ge(s_exp, g + (NG * l + 1))
                    for j in range(jj * G, (jj + 1) * G):
                        z = rows3[:, j, 0:D].rearrange("p (h d) -> p h d", h=H)
                        a = rows3[:, j, D:w].unsqueeze(2).broadcast_to([P, H, D // H])
                        nc.vector.tensor_tensor(z, z, a, ALU.mult).then_inc(s_msg, 1)

                def close_blocks(g):
                    lo = dve.value_load(b_k[0:1, bass.ds(g * G, 1)], min_val=0, max_val=NB)
                    hi = dve.value_load(b_k[0:1, bass.ds(g * G + G, 1)], min_val=0, max_val=NB)
                    with dve.If(lo < hi):
                        with dve.Fori(lo, hi) as b:
                            close(b)

                def close(b):
                    end = dve.value_load(ends[0:1, bass.ds(b, 1)], min_val=0, max_val=V)
                    dve.wait_ge(s_agg, end + (V * l + AHEAD))
                    odd = (b + l) % 2
                    flat = PS[:, :, :].rearrange("p b n -> p (b n)")
                    at = flat[:, bass.ds(odd * 1024, 1024)].rearrange("p (c n) -> p c n", c=2)
                    steps = []
                    den = at[:, 1, HALF:HALF + H]
                    nc.vector.tensor_scalar(rec[:, 0, 0:H], den, 0.5, None, ALU.max).then_inc(s_close, 1)
                    dve.wait_ge(s_close, b * 3 + (3 * NB * l + 1))
                    nc.vector.reciprocal(rec[:, 1, 0:H], rec[:, 0, 0:H]).then_inc(s_close, 1)
                    dve.wait_ge(s_close, b * 3 + (3 * NB * l + 2))
                    dve.wait_ge(s_sums_free, b + (NB * l + 1))
                    to = sums[:, :, :].rearrange("p q n -> p (q n)")[:, bass.ds(odd * D, D)]
                    for c in range(2):
                        hh = H // 2 if H > 1 else 1
                        r = rec[:, 1, c * hh:(c + 1) * hh] if H > 1 else rec[:, 1, 0:1]
                        o = nc.vector.tensor_tensor(
                            to[:, c * HALF:(c + 1) * HALF].rearrange("p (h d) -> p h d", h=hh),
                            at[:, c, 0:HALF].rearrange("p (h d) -> p h d", h=hh),
                            r.unsqueeze(2).broadcast_to([P, hh, HALF // hh]), ALU.mult)
                        o.then_inc(s_close if c == 0 else s_sums, 1)
                    dve.wait_ge(s_close, b * 3 + (3 * NB * l + 3))
                    dve.wait_ge(s_sums, b + (NB * l + 1))
                    dve.sem_inc(s_tick_dve)
                    nc.vector.tensor_copy(at[:, :, 0:HALF + H],
                                          zeros[:, 0:2 * (HALF + H)].rearrange("p (c n) -> p c n", c=2)).then_inc(s_acc_free, 1)

                def body(i, last):
                    for jj in range(NBUF):
                        g = NBUF * i + jj
                        exponents(g, i, jj)
                        if not (last and jj == NBUF - 1):
                            one_hots(g + 1, (jj + 1) % NBUF)
                        weigh(g, jj)
                        if jj or not isinstance(i, int) or i:
                            close_blocks(g - 1)

                one_hots(0, 0)
                body(0, False)
                with dve.Fori(1, NI - 1) as i:
                    dc.enter(i - 1, 3 * NBUF)
                    body(i, False)
                dc.leave(NI - 2)
                body(NI - 1, True)
                close_blocks(NG - 1)

            for l in range(3):
                node_sweep(l)
                edge_sweep(l)

            dve.wait_ge(s_wT, 25)
            nc.vector.tensor_copy(WrT[:, :], PS[:, 2, 0:KC * EX]).then_inc(s_wcp, 1)
            nc.vector.tensor_copy(bi_col[:, :], PS[:, 3, 0:FC]).then_inc(s_wcp, 1)

            def begin(b):
                in_ready(b, 3)
                free_again(dve, b, s_xTp, 3)
                free_again(dve, b, s_or, 0)
                u = in0(b.q)
                link(nc.vector.tensor_tensor(u, u, in1(b.q), ALU.add))
                link(nc.vector.tensor_tensor(u, u, bias[:, :], ALU.add))
                link(nc.vector.tensor_tensor(x2(b.q), u, in2(b.q), ALU.add))
                link(layernorm(b, x2(b.q), 3, None))
                dve.sem_inc(s_rows, 1)
                dve.sem_inc(s_in_used, 1)

            def gates(b):
                dve.wait_ge(s_lg, b.n + 1)
                if b.reuse or b.n:
                    dve.wait_ge(s_gTp, b.n)
                lg, top = gate[:, 8:16], gate[:, 16:24]
                link(nc.vector.tensor_copy(lg, PS[:, 7, 0:EX]))
                dve.sem_inc(s_tick_dve)
                link(nc.vector.max(top, lg))
                dve.sem_inc(s_tick_dve)
                link(nc.vector.max_index(gate_i[:, :], top, lg))
                nc.vector.tensor_tensor(gate[:, 0:1], top[:, 1:2], top[:, 0:1], ALU.subtract).then_inc(s_d, 1)
                link(nc.vector.tensor_copy(gate[:, 24:32], gate_i[:, :]))
                dve.wait_ge(s_e, b.n + 1)
                link(nc.vector.tensor_scalar(gate[:, 2:3], gate[:, 1:2], 1.0, None, ALU.add))
                link(nc.vector.reciprocal(gate[:, 3:4], gate[:, 2:3]))
                link(nc.vector.tensor_tensor(gate[:, 4:5], gate[:, 1:2], gate[:, 3:4], ALU.mult))
                link(nc.vector.tensor_scalar(gate[:, 40:48], iota_row[:, 0:EX], gate[:, 24:25], gate[:, 3:4],
                                             ALU.is_equal, ALU.mult))
                link(nc.vector.tensor_scalar(gate[:, 48:56], iota_row[:, 0:EX], gate[:, 25:26], gate[:, 4:5],
                                             ALU.is_equal, ALU.mult))
                link(nc.vector.tensor_tensor(gate[:, 32:40], gate[:, 40:48], gate[:, 48:56], ALU.add))
                dve.sem_inc(s_g, 1)
                for grp in range(3):
                    m = 3 * b.n + grp
                    dve.wait_ge(s_gelu, m + 1)
                    dve.wait_ge(s_gx, m + 1)
                    if grp == 0 and (b.reuse or b.n):
                        dve.wait_ge(s_op, b.n)
                    half = (b.q + grp) % 2
                    nc.vector.tensor_tensor(hg[:, grp * 512:(grp + 1) * 512], hid[:, half * 512:(half + 1) * 512],
                                            PS[:, 4, :], ALU.mult).then_inc(s_hg, 1)
            def result(b):
                dve.wait_ge(s_op, b.n + 1)
                if b.reuse:
                    dve.wait_ge(s_or_st[b.q], 16 * b.turn)
                nc.vector.tensor_tensor(zr(b.q, D), x2(b.q), flat_banks(5)[:, 0:D], ALU.add).then_inc(s_or, 1)

            dve.wait_ge(s_bias, 16 * 3)
            sweep_nodes(dve, [(gates, 0), (begin, 1), (result, 0)], dc, 2 * (3 + 3 + 10))


_INS = ["x", "src", "dst"] + [f"L0_gnn_{n}{i}" for i in range(3) for n in ("W", "al", "ar", "b")] + [
    f"L0_ffn_{n}" for n in ("Wr", "Wi", "bi", "Wo", "bo")]


def kernel(**inputs):
    import numpy as _np
    import concourse.bacc as _bacc
    from concourse.bass_utils import run_bass_kernel_spmd as _run

    nc = _bacc.Bacc("TRN2", target_bir_lowering=False, num_devices=1)
    arrays, args = {}, {}
    for name in _INS:
        a = _np.ascontiguousarray(inputs[name])
        arrays[f"in_{name}"] = a
        args[name] = nc.dram_tensor(f"in_{name}", a.shape, mybir.dt.from_np(a.dtype), kind="ExternalInput").ap()
    out = nc.dram_tensor("out_0", (N, D), F32, kind="ExternalOutput").ap()
    gnn = [{n: args[f"L0_gnn_{n}{i}"] for n in ("W", "al", "ar", "b")} for i in range(3)]
    ffn = {n: args[f"L0_ffn_{n}"] for n in ("Wr", "Wi", "bi", "Wo", "bo")}
    gnn_ffn(nc, args["x"], args["src"], args["dst"], gnn, ffn, out)
    r = _run(nc, [arrays], core_ids=[0])
    return r.results[0]["out_0"]
```

```python
from contextlib import ExitStack

import concourse.bass as bass
from concourse import mybir

F32 = mybir.dt.float32
BF16 = mybir.dt.bfloat16
I32 = mybir.dt.int32
U32 = mybir.dt.uint32
ALU = mybir.AluOpType
ACT = mybir.ActivationFunctionType
AX_X = mybir.AxisListType.X

P = 128
N, D = 3125, 768
NE = 50000
NB = -(-N // P)
NPAD = NB * P
LAST = N - (NB - 1) * P
KC = D // P
ET = -(-NE // P)
HEADS = (12, 12, 1)
HMAX = max(HEADS)
G = 5
NBUF = 3
U = G * NBUF
V = -(-(ET + NB - 1) // U) * U
NG = V // G
NI = NG // NBUF
ROW = D + HMAX
HALF = D // 2
EX, FF = 8, 192
F = EX * FF
FH = FF // 2
TOP = 2
NS = (TOP * N + EX * (P - 1)) // P
NO_NODE = -1.0
SLOPE = 0.2
EPS = 1e-5


class Chain:

    def __init__(self, eng, sem):
        self.eng, self.sem, self.base, self.turns = eng, sem, 0, 0

    def link(self, instruction):
        instruction.then_inc(self.sem, 1)
        self.base += 1
        self.eng.wait_ge(self.sem, self.base + self.turns)

    def enter(self, turn, per):
        self.start, self.per, self.turns = self.base, per, turn * per

    def leave(self, trips):
        assert self.base - self.start == self.per, (self.base - self.start, self.per)
        self.turns, self.base = 0, self.start + trips * self.per


class Block:

    def __init__(self, c, i=None):
        self.q = c % 2
        self.n = c if i is None else i * 2 + c
        self.turn = c // 2 if i is None else i + c // 2
        self.reuse = i is not None or c >= 2
        self.rows = LAST if i is None and c == NB - 1 else P
        self.fixed = i is None

    def row0(self):
        return self.n * P


def gnn_ffn(nc, x, src, dst, gnn, ffn, out):
    with ExitStack() as ctx:
        def sb(name, shape, dt=F32):
            return ctx.enter_context(nc.sbuf_tensor(name, shape, dt))

        def sem(name):
            return ctx.enter_context(nc.semaphore(name))

        edges = nc.dram_tensor("edges", (ET, 2 * P), I32, kind="Internal").ap()
        table = [nc.dram_tensor(f"table{l}", (NPAD, D + h), F32, kind="Internal").ap() for l, h in enumerate(HEADS)]
        normed = nc.dram_tensor("normed", (NPAD, D), F32, kind="Internal").ap()
        x2_kept = nc.dram_tensor("x2_kept", (NPAD, D), F32, kind="Internal").ap()
        expert_out = nc.dram_tensor("expert_out", (NS * P, D), F32, kind="Internal").ap()
        mixed = [nc.dram_tensor(f"mixed{l}", (NPAD, D), F32, kind="Internal").ap() for l in range(3)]

        PS = ctx.enter_context(nc.psum_tensor("PS", [P, 8, 512], F32))
        arena = sb("arena", [P, U * ROW])
        W = sb("W", [P, 3, KC, D + 2 * HMAX])
        WoT = sb("WoT", [P, EX, 2, D])
        WrT = sb("WrT", [P, KC * EX])
        Wr_rows = sb("Wr_rows", [EX, D])
        bias = sb("bias", [P, D])
        WiT = W[:, :, :, :].rearrange("p l k n -> p (l k n)")[:, 0:KC * F].rearrange("p (k f) -> p k f", k=KC)
        W_rest = W[:, :, :, :].rearrange("p l k n -> p (l k n)")[:, KC * F:]
        bi_row = W_rest[0:1, 0:F]
        earlier = sb("earlier", [P, P])
        token_i = sb("token_i", [P, NB], I32)
        token_of = sb("token_of", [P, NS], I32)
        place_of = sb("place_of", [P, NB, TOP], I32)
        expert_at = sb("expert_at", [1, NS // 2, 4], I32)
        chosen = sb("chosen", [P, 4], I32)
        ident = sb("ident", [P, P])
        ones = sb("ones", [P, P])
        zeros = sb("zeros", [P, D + 2 * HMAX])
        zeros_h = sb("zeros_h", [P, 512], BF16)
        iota_row = sb("iota_row", [P, P])
        iota_i = sb("iota_i", [P, V], I32)
        eps = sb("eps", [P, 2])
        src_k = sb("src_k", [P, V], I32)
        dst_k = sb("dst_k", [P, V])
        b_k = sb("b_k", [1, V + 1], I32)
        b_g = sb("b_g", [1, NG, 12], I32)
        ends = sb("ends", [1, NB], I32)
        erm = sb("erm", [P, NB, 2 * HMAX])
        ert = sb("ert", [P, NB, HMAX])
        gm = sb("gm", [P, HMAX])
        gmb = sb("gmb", [P, 2, HMAX])
        S = sb("S", [P, NBUF, G, P])
        ST = sb("ST", [P, NBUF, G, P])
        wt = sb("wt", [P, NBUF, G, HMAX])
        wu = sb("wu", [P, NBUF, G, HMAX])
        stage = sb("stage", [P, U], I32)
        sums = sb("sums", [P, 2, D])
        rec = sb("rec", [P, 2, HMAX])
        stats = sb("stats", [P, 2, 16])
        gate = sb("gate", [P, 96])

        def rows_buf(j, q, width=D):
            return arena[:, (2 * j + q) * D:(2 * j + q) * D + width]

        def zr(q, width):
            return arena[:, 12 * D + q * (D + 2 * HMAX):12 * D + q * (D + 2 * HMAX) + width]

        in0, in1, in2, xr, xT, x2 = (lambda q, j=j: rows_buf(j, q) for j in range(6))

        s_const = sem("s_const"); s_cload = sem("s_cload"); s_pad = sem("s_pad"); s_dst = sem("s_dst")
        s_prep = sem("s_prep"); s_cnt = sem("s_cnt"); s_tk = sem("s_tk"); s_tki = sem("s_tki")
        s_rows_k = sem("s_rows_k"); s_rows_f = sem("s_rows_f"); s_turned = sem("s_turned"); s_tables = sem("s_tables")
        s_w = [sem(f"s_w{l}") for l in range(3)]; s_waug = sem("s_waug"); s_al = sem("s_al"); s_al_used = sem("s_al_used")
        s_wld = [sem("s_wld0"), sem("s_wld1")]; s_wol = [sem("s_wol0"), sem("s_wol1")]; s_wT = sem("s_wT"); s_wcp = sem("s_wcp"); s_bias = sem("s_bias")
        s_in = [sem("s_in0"), sem("s_in1")]
        s_in_used = sem("s_in_used"); s_stat = sem("s_stat"); s_std = sem("s_std")
        s_rows = sem("s_rows"); s_xTp = sem("s_xTp"); s_xT = sem("s_xT"); s_zp = sem("s_zp"); s_zr = sem("s_zr")
        s_tab = sem("s_tab"); s_stored = [sem("s_stored0"), sem("s_stored1")]
        s_gmT = sem("s_gmT"); s_diag = sem("s_diag"); s_gmB = sem("s_gmB"); s_erm = sem("s_erm")
        s_staged = sem("s_staged"); s_tick = sem("s_tick")
        s_z = [sem(f"s_z{j}") for j in range(U)]
        s_S = sem("s_S"); s_STp = sem("s_STp"); s_ST = sem("s_ST"); s_er = sem("s_er"); s_pre = sem("s_pre")
        s_exp = sem("s_exp"); s_msg = sem("s_msg"); s_agg = sem("s_agg"); s_acc_free = sem("s_acc_free")
        s_sums = sem("s_sums"); s_sums_free = sem("s_sums_free"); s_sums_st = sem("s_sums_st")
        s_lg = sem("s_lg"); s_kept = [sem("s_kept0"), sem("s_kept1")]; s_kept_x2 = [sem("s_kept_x20"), sem("s_kept_x21")]
        s_d = sem("s_d"); s_e = sem("s_e"); s_pairs = sem("s_pairs"); s_ranks = sem("s_ranks")
        s_onehots = sem("s_onehots"); s_tokens_p = sem("s_tokens_p"); s_routed = sem("s_routed")
        s_xg = [sem("s_xg0"), sem("s_xg1")]; s_chosen = sem("s_chosen"); s_xgTp = sem("s_xgTp"); s_xgT = sem("s_xgT")
        s_up = sem("s_up"); s_gelu = sem("s_gelu"); s_hTp = sem("s_hTp"); s_hT = sem("s_hT"); s_down = sem("s_down")
        s_y = sem("s_y"); s_y_st = [sem("s_y_st0"), sem("s_y_st1")]
        s_ab = [sem("s_ab0"), sem("s_ab1")]; s_x2in = [sem("s_x2in0"), sem("s_x2in1")]; s_or = sem("s_or")
        s_or_st = [sem("s_or_st0"), sem("s_or_st1")]
        s_dve = sem("s_dve"); s_acts = sem("s_acts"); s_pool = sem("s_pool"); s_close = sem("s_close"); s_tick_dve = sem("s_tick_dve")

        AHEAD = U

        def sweep_nodes(eng, stages, chain=None, per=0, count=NB):
            def steps(i, ts):
                for t in ts:
                    for stage, lead in stages:
                        if i is not None or 0 <= t + lead < count:
                            stage(Block(t + lead, i))

            steps(None, range(-max(lead for _, lead in stages), 2))
            trips = (count - 4) // 2
            with eng.Fori(1, 1 + trips) as i:
                if chain:
                    chain.enter(i - 1, per)
                steps(i, (0, 1))
            if chain:
                chain.leave(trips)
            steps(None, range(2 + 2 * trips, count - min(lead for _, lead in stages)))

        def free_again(eng, b, sem, l):
            if b.reuse:
                eng.wait_ge(sem, b.n + (NB * l - 1))

        def z_width(l):
            return D + 2 * HEADS[l]

        def flat_banks(b):
            return PS[:, b:b + 2, :].rearrange("p b n -> p (b n)")

        def edge_heads(l, jj):
            w = D + HEADS[l]
            return arena[:, 0:U * w].rearrange("p (u n) -> p u n", u=U)[:, jj * G:(jj + 1) * G, D:w]

        def bk_f():
            return arena[:, 9700:9700 + V]

        def ert_flat(l):
            return ert[:, :, :].rearrange("p b h -> p (b h)")[:, 0:NB * HEADS[l]]

        def wcount():
            return arena[0:125, 400 * 24:401 * 24]

        def tk_row():
            return arena[0:1, U * ROW - V:U * ROW]

        def rows_f():
            return arena[:, 4 * 2 * P:8 * 2 * P]

        def wo_rows(h):
            return arena[:, (4 + 2 * (h % 2)) * D:(6 + 2 * (h % 2)) * D]

        sizes = dict.fromkeys(("lg", "pairs", "t", "one0", "one1", "upto", "other"), NB * EX)
        sizes |= dict.fromkeys(("best", "v0", "v1", "d", "e", "g0", "g1", "token", "real"), NB)
        sizes |= dict.fromkeys(("place", "slot"), NB * TOP)
        sizes |= dict.fromkeys(("rising", "slots", "last_slot", "swap", "slots_i"), EX)
        sizes["expert"] = NS

        def routing(name):
            at = F
            for n, size in sizes.items():
                if n == name:
                    return W_rest[:, at:at + size]
                at += size

        def at_place():
            return arena[:, 0:NB * TOP * P].rearrange("p (m n) -> p m n", n=P)

        def at_slot():
            return arena[:, NB * TOP * P:NB * TOP * (P + NS)].rearrange("p (m n) -> p m n", n=NS)

        def ended_at():
            return arena[0:1, NB * TOP * (P + NS):NB * TOP * (P + NS) + NS * EX].rearrange("o (s e) -> o s e", e=EX)

        def h_rows(q):
            return in1(q)[:, 0:FF]

        def hT(q):
            return in2(q)[:, 0:2 * P]

        def erm_flat(l):
            return erm[:, :, :].rearrange("p b h -> p (b h)")[:, 0:NB * 2 * HEADS[l]]

        block = ctx.enter_context(nc.Block())

        @block.sync
        def _(sp):
            flat_S = S[:, :, :, :].rearrange("p a b c -> p (a b c)")
            sp.dma_start(flat_S[0:125, 0:400].bitcast(I32), dst.rearrange("(p e) -> p e", p=125)).then_inc(s_dst, 16)
            full = NE // P * P
            sp.dma_start(edges[0:ET - 1, 0:P], src[0:full].rearrange("(t e) -> t e", e=P)).then_inc(s_pad, 16)
            sp.dma_start(edges[0:ET - 1, P:2 * P], dst[0:full].rearrange("(t e) -> t e", e=P)).then_inc(s_pad, 16)
            sp.dma_start(edges[ET - 1:ET, 0:NE - full], src[full:NE].rearrange("(t e) -> t e", t=1)).then_inc(s_pad, 16)
            sp.dma_start(edges[ET - 1:ET, P:P + NE - full], dst[full:NE].rearrange("(t e) -> t e", t=1)).then_inc(s_pad, 16)
            sp.wait_ge(s_const, 3)
            pad = P - (NE - full)
            sp.dma_start(edges[ET - 1:ET, NE - full:P], src_k[0:1, 0:pad]).then_inc(s_pad, 16)
            sp.dma_start(edges[ET - 1:ET, P + NE - full:2 * P], src_k[0:1, P:P + pad]).then_inc(s_pad, 16)

            def load(l):
                last = l == 3

                def begin(b):
                    free_again(sp, b, s_in_used, l)
                    ins = []
                    if l == 0 or last:
                        to = in2 if last else in0
                        ins.append((to(b.q)[0:b.rows], x[bass.ds(b.row0(), b.rows), :]))
                    if l:
                        ins.append((in0(b.q), mixed[l - 1][bass.ds(b.row0(), P), :]))
                        ins.append((in1(b.q), table[l - 1][bass.ds(b.row0(), P), 0:D]))
                    for o, i in ins:
                        sp.dma_start(o, i).then_inc(s_in[b.q], 16)
                return begin

            for l in range(4):
                if l == 0:
                    sp.wait_ge(s_waug, 3)
                if l:
                    sp.wait_ge(s_sums_st, 16 * NB * l)
                    sp.dma_start(bias[:, :], gnn[3 * 0 + l - 1]["b"].partition_broadcast(P)).then_inc(s_bias, 16)
                sweep_nodes(sp, [(load(l), 0)])
                if l == 2:
                    sp.wait_ge(s_stored[0], 16 * (NB // 2 + 1) * 3)
                    sp.wait_ge(s_stored[1], 16 * (NB // 2) * 3)
                    for u in range(12):
                        if u >= 2:
                            sp.wait_ge(s_wT, u - 1)
                        sp.dma_start(rows_buf(u % 2, 0), ffn["Wi"].rearrange("e f d -> (e f) d")[u * P:(u + 1) * P, :]).then_inc(s_wld[u % 2], 16)
                    for h in range(KC):
                        if h >= 2:
                            sp.wait_ge(s_wT, 12 + 2 * (h - 1))
                        sp.dma_start(wo_rows(h).rearrange("p (e f) -> p e f", e=EX),
                                     ffn["Wo"][:, h * P:(h + 1) * P, :].rearrange("e p f -> p e f")).then_inc(s_wol[h % 2], 16)
                if l < 3:
                    def sums_out(n, q):
                        sp.wait_ge(s_sums, n + (NB * l + 1))
                        sp.dma_start(mixed[l][bass.ds(n * P, P), :],
                                     sums[:, q, :]).then_inc(s_sums_st, 16)
                        sp.wait_ge(s_sums_st, 16 * n + 16 * (NB * l + 1))
                        sp.sem_inc(s_sums_free, 1)
                    with sp.Fori(0, NB // 2) as i:
                        for c in (0, 1):
                            sums_out(i * 2 + c, (NB * l + c) % 2)
                    sums_out(NB - 1, (NB * l + NB - 1) % 2)

            def store_y(b):
                sp.wait_ge(s_y, b.n + 3)
                sp.dma_start(expert_out[bass.ds(b.row0(), P), :], zr(b.q, D)).then_inc(s_y_st[b.q], 16)

            def load_x2(b):
                if b.reuse:
                    sp.wait_ge(s_or, b.n - 1)
                sp.dma_start(x2(b.q), x2_kept[bass.ds(b.row0(), P), :]).then_inc(s_x2in[b.q], 16)

            sweep_nodes(sp, [(store_y, 0)], count=NS)
            sweep_nodes(sp, [(load_x2, 0)])

        @block.gpsimd
        def _(pool):
            pc = Chain(pool, s_pool)
            pc.link(nc.gpsimd.memset(src_k[0:1, 0:P], 0))
            nc.gpsimd.memset(src_k[0:1, P:2 * P], int(NO_NODE)).then_inc(s_const, 3)
            pc.link(nc.gpsimd.memset(ident[:, :], 0.0))
            nc.gpsimd.affine_select(out=ident[:, :], in_=ident[:, :], compare_op=ALU.not_equal, fill=1.0, base=0,
                                    pattern=[[-1, P]], channel_multiplier=1).then_inc(s_const, 1)
            nc.gpsimd.memset(ones[:, :], 1.0).then_inc(s_const, 1)
            nc.gpsimd.memset(zeros[:, :], 0.0).then_inc(s_const, 1)
            nc.gpsimd.memset(zeros_h[:, :], 0.0).then_inc(s_const, 1)
            nc.gpsimd.memset(eps[:, 0:1], EPS).then_inc(s_const, 1)
            nc.gpsimd.memset(eps[:, 1:2], -1.0).then_inc(s_const, 1)
            nc.gpsimd.iota(iota_i[:, :], pattern=[[1, V]], base=0, channel_multiplier=0).then_inc(s_const, 1)
            pc.link(nc.gpsimd.iota(token_i[:, :], pattern=[[P, NB]], base=0, channel_multiplier=1))
            pc.link(nc.gpsimd.memset(earlier[:, :], 1.0))
            nc.gpsimd.affine_select(out=earlier[:, :], in_=earlier[:, :], compare_op=ALU.is_ge, fill=0.0,
                                    base=-1, pattern=[[1, P]], channel_multiplier=-1).then_inc(s_const, 1)

            ek = arena[:, 0:4 * 2 * P].bitcast(I32)
            tki = gate[:, 0:4].bitcast(U32)
            pool.wait_ge(s_pad, 16 * 6)
            pool.wait_ge(s_tki, 2)
            pool.sem_inc(s_tick)
            for c in range(4):
                n = min(P, V - c * P)
                nc.gpsimd.indirect_dma_start(ek[0:n, c * 2 * P:(c + 1) * 2 * P], None, edges[:, :],
                                             bass.IndirectOffsetOnAxis(tki[0:n, c:c + 1], 0)).then_inc(s_rows_k, 16)

            def store(l):
                def run(b):
                    pool.wait_ge(s_zr, b.n + (NB * l + 1))
                    pool.sem_inc(s_tick)
                    nc.gpsimd.dma_start(table[l][bass.ds(b.row0(), P), :],
                                        zr(b.q, D + HEADS[l])).then_inc(s_stored[b.q], 16)
                return run

            def keep_rows(b):
                pool.wait_ge(s_rows, b.n + (NB * 3 + 1))
                pool.sem_inc(s_tick)
                nc.gpsimd.dma_start(normed[bass.ds(b.row0(), P), :], xr(b.q)).then_inc(s_kept[b.q], 16)

            def gather_tokens(b):
                if b.reuse:
                    pool.wait_ge(s_xgTp, b.n - 1)
                pool.sem_inc(s_tick)
                nc.gpsimd.tensor_copy(chosen[:, b.q:b.q + 1], token_of[:, bass.ds(b.n, 1)]).then_inc(s_chosen, 1)
                pool.wait_ge(s_chosen, b.n + 1)
                pool.sem_inc(s_tick)
                nc.gpsimd.indirect_dma_start(in0(b.q), None, normed[:, :], bass.IndirectOffsetOnAxis(
                    chosen[:, b.q:b.q + 1].bitcast(U32), 0)).then_inc(s_xg[b.q], 16)

            def gather_pairs(b):
                if b.reuse:
                    pool.wait_ge(s_or, b.n - 1)
                pool.sem_inc(s_tick)
                at = slice(2 * b.q, 2 * b.q + 2)
                nc.gpsimd.tensor_copy(chosen[:, at], place_of[:, :, :].rearrange("p b j -> p (b j)")[
                    :, bass.ds(b.n * TOP, TOP)]).then_inc(s_chosen, 1)
                pool.wait_ge(s_chosen, b.n + (NS + 1))
                pool.sem_inc(s_tick)
                for j, to in enumerate((in0(b.q), in1(b.q))):
                    nc.gpsimd.indirect_dma_start(to, None, expert_out[:, :], bass.IndirectOffsetOnAxis(
                        chosen[:, 2 * b.q + j:2 * b.q + j + 1].bitcast(U32), 0)).then_inc(s_ab[b.q], 16)

            for l in range(3):
                sweep_nodes(pool, [(store(l), 0)])
                pool.wait_ge(s_stored[0], 16 * (NB // 2 + 1) * (l + 1))
                pool.wait_ge(s_stored[1], 16 * (NB // 2) * (l + 1))
                pool.wait_ge(s_tab, NB * (l + 1))
                pool.wait_ge(s_tables, 1)
                if l == 2:
                    pool.wait_ge(s_wT, 24)
                pool.sem_inc(s_tick)
                with pool.Fori(0, NI) as i:
                    for jj in range(NBUF):
                        pool.wait_ge(s_agg, U * i + (G * (jj + 1) + V * l))
                        pool.sem_inc(s_tick)
                        nc.gpsimd.tensor_copy(stage[:, jj * G:(jj + 1) * G],
                                              src_k[:, bass.ds(i * U + jj * G, G)]).then_inc(s_staged, 1)
                        pool.wait_ge(s_staged, NBUF * i + (jj + 1 + NG * l))
                        pool.sem_inc(s_tick)
                        for j in range(jj * G, (jj + 1) * G):
                            w = D + HEADS[l]
                            nc.gpsimd.indirect_dma_start(
                                arena[:, j * w:(j + 1) * w], None, table[l][:, :],
                                bass.IndirectOffsetOnAxis(stage[:, j:j + 1].bitcast(U32), 0)).then_inc(s_z[j], 16)

            sweep_nodes(pool, [(keep_rows, 0)])
            for q in range(2):
                pool.wait_ge(s_kept[q], 16 * (NB // 2 + 1 - q))
            pool.wait_ge(s_routed, 1)
            sweep_nodes(pool, [(gather_tokens, 0)], count=NS)
            for q in range(2):
                pool.wait_ge(s_y_st[q], 16 * (NS // 2 + 1))
            sweep_nodes(pool, [(gather_pairs, 0)])

        @block.scalar
        def _(act):
            ac = Chain(act, s_acts)
            for l in range(3):
                act.dma_start(W[:, l, :, 0:D], gnn[l]["W"].rearrange("(k p) n -> p k n", p=P)).then_inc(s_w[l], 16)
            act.dma_start(WoT[FH:FH + 1, :, 1, :], ffn["bo"].rearrange("(o e) d -> o e d", o=1)).then_inc(s_cload, 16)
            act.dma_start(Wr_rows[:, :], ffn["Wr"]).then_inc(s_cload, 16)
            albc = [arena[:, (8 + j) * D:(9 + j) * D] for j in range(2)]
            for l in range(3):
                if l:
                    act.wait_ge(s_al_used, l)
                else:
                    act.wait_ge(s_prep, 3)
                for j, name in enumerate(("al", "ar")):
                    act.dma_start(albc[j], gnn[l][name].rearrange("h d -> (h d)").partition_broadcast(P)).then_inc(s_al, 16)

            def make_xT(l, banks):
                def xt(b):
                    act.wait_ge(s_xTp, b.n + (NB * l + 1))
                    free_again(act, b, s_zp if l < 3 else s_lg, l % 3)
                    nc.scalar.activation(xT(b.q), banks(b.q)[:, 0:D], ACT.Copy).then_inc(s_xT, 1)
                return xt

            def std(b, k):
                act.wait_ge(s_stat, b.n + (NB * k + 1))
                nc.scalar.activation(stats[:, b.q, 14:15], stats[:, b.q, 13:14], ACT.Sqrt,
                                     bias=eps[:, 0:1]).then_inc(s_std, 1)

            def node_sweep(l):
                xt = make_xT(l, lambda q: flat_banks(2 * q))

                def finish_rows(b):
                    if l == 0:
                        std(b, 0)
                    else:
                        act.wait_ge(s_stat, b.n + (NB * l + 1))
                        ac.link(nc.scalar.activation(in1(b.q), in1(b.q), ACT.Exp))
                        nc.scalar.activation(in1(b.q), in1(b.q), ACT.Identity, bias=eps[:, 1:2]).then_inc(s_std, 1)

                def copy_z(b):
                    act.wait_ge(s_zp, b.n + (NB * l + 1))
                    if b.reuse:
                        act.wait_ge(s_stored[b.q], 16 * b.turn + 16 * (NB // 2 + (1 - b.q)) * l)
                    free_again(act, b, s_tab, l)
                    nc.scalar.activation(zr(b.q, z_width(l)), flat_banks(4 + 2 * b.q)[:, 0:z_width(l)],
                                         ACT.Copy).then_inc(s_zr, 1)

                sweep_nodes(act, [(finish_rows, 2), (xt, 1), (copy_z, 0)], ac if l else None, 2)

            def ffn_weights():
                for u in range(24):
                    if u < 12:
                        to = WiT[:, :, u * P:(u + 1) * P]
                    else:
                        h, half = divmod(u - 12, 2)
                        to = WoT[0:FH, 4 * half:4 * half + 4, :, h * P:(h + 1) * P].rearrange("f e j d -> f (e j) d")
                    act.wait_ge(s_wT, u + 1)
                    turned = flat_banks(2 * (u % 2))
                    turned = (turned[:, 0:D] if u < 12 else turned[0:FH, :]).rearrange("p (k f) -> p k f", f=P)
                    nc.scalar.activation(to, turned, ACT.Copy).then_inc(s_wcp, 1)
                    if u == 0:
                        act.dma_start(bi_row, ffn["bi"].rearrange("e f -> (e f)").rearrange("(o n) -> o n", o=1)).then_inc(s_cload, 16)

            def edge_sweep(l):
                H = HEADS[l]

                def copy_ST(g, jj):
                    act.wait_ge(s_STp, g + (NG * l + 1))
                    nc.scalar.activation(ST[:, jj, :, :].rearrange("p g e -> p (g e)"), flat_banks(4)[:, 0:G * P],
                                         ACT.Copy).then_inc(s_ST, 1)

                def body(i, last):
                    for jj in range(NBUF):
                        g = NBUF * i + jj
                        act.wait_ge(s_pre, g + (NG * l + 1))
                        nc.scalar.activation(edge_heads(l, jj), wt[:, jj, :, 0:H], ACT.Exp).then_inc(s_exp, 1)
                        if not (last and jj == NBUF - 1):
                            copy_ST(g + 1, (jj + 1) % NBUF)

                copy_ST(0, 0)
                with act.Fori(0, NI - 1) as i:
                    body(i, False)
                body(NI - 1, True)

            for l in range(3):
                node_sweep(l)
                if l == 2:
                    ffn_weights()
                edge_sweep(l)

            xt = make_xT(3, lambda q: flat_banks(0))

            def keep_x2(b):
                act.wait_ge(s_rows, b.n + (NB * 3 + 1))
                act.dma_start(x2_kept[bass.ds(b.row0(), P), :], x2(b.q)).then_inc(s_kept_x2[b.q], 16)

            sweep_nodes(act, [(lambda b: std(b, 3), 2), (xt, 1), (keep_x2, 1)])
            act.wait_ge(s_d, 1)
            nc.scalar.activation(routing("e"), routing("d"), ACT.Exp).then_inc(s_e, 1)

            def gelu(b):
                act.wait_ge(s_up, b.n + 1)
                if b.reuse:
                    act.wait_ge(s_hTp, b.n - 1)
                nc.scalar.activation(h_rows(b.q), PS[:, 2, b.q * 256:b.q * 256 + FF], ACT.Gelu).then_inc(s_gelu, 1)

            def copy_xT(b):
                act.wait_ge(s_xgTp, b.n + 1)
                if b.reuse:
                    act.wait_ge(s_up, b.n - 1)
                nc.scalar.activation(xT(b.q), flat_banks(0)[:, 0:D], ACT.Copy).then_inc(s_xgT, 1)

            def store_out(b):
                act.wait_ge(s_or, b.n + 1)
                act.dma_start(out[bass.ds(b.row0(), b.rows), :], zr(b.q, D)[0:b.rows]).then_inc(s_or_st[b.q], 16)

            sweep_nodes(act, [(gelu, 0), (copy_xT, 1)], count=NS)
            sweep_nodes(act, [(store_out, 0)])
            for q in range(2):
                act.wait_ge(s_or_st[q], 16 * (NB // 2 + 1 - q))
                act.wait_ge(s_kept_x2[q], 16 * (NB // 2 + 1 - q))

        @block.tensor
        def _(pe):
            pe.sem_inc(s_agg, AHEAD)
            pe.sem_inc(s_acc_free, 2)
            pe.sem_inc(s_sums_free, 2)
            pe.sem_inc(s_y, 2)
            for q in range(2):
                pe.sem_inc(s_y_st[q], 16)
            pe.wait_ge(s_const, 11)
            pe.wait_ge(s_prep, 1)
            nc.tensor.matmul(PS[:, 0, 0:NB - 1], ones[0:125, :], wcount(), start=True, stop=True).then_inc(s_cnt, 1)
            pe.wait_ge(s_prep, 2)
            for c in range(4):
                n = min(P, V - c * P)
                last = nc.tensor.matmul(PS[0:n, 1, c:c + 1], tk_row()[:, c * P:c * P + n], ones[0:1, 0:1],
                                        start=True, stop=True)
            last.then_inc(s_tk, 1)
            pe.wait_ge(s_rows_f, 1)
            for j in range(2):
                for c in range(4):
                    n = min(P, V - c * P)
                    last = nc.tensor.transpose(PS[:, 2 + j, c * P:c * P + n],
                                               rows_f()[0:n, (2 * c + j) * P:(2 * c + j + 1) * P], ident[0:n, 0:n])
            last.then_inc(s_turned, 1)

            def turn_rows(l, banks):
                def turn(b):
                    pe.wait_ge(s_rows, b.n + (NB * l + 1))
                    if l < 3:
                        free_again(pe, b, s_xT, l)
                    elif b.reuse or b.n:
                        pe.wait_ge(s_xT, b.n + NB * l)
                    for k in range(KC):
                        o = nc.tensor.transpose(banks(b.q)[:, k * P:(k + 1) * P], xr(b.q)[:, k * P:(k + 1) * P],
                                                ident[:, :])
                    o.then_inc(s_xTp, 1)
                return turn

            def node_sweep(l):
                def product(b, ks):
                    for k in ks:
                        lhsT = xT(b.q)[:, k * P:(k + 1) * P]
                        nc.tensor.matmul(PS[:, 4 + 2 * b.q, :], lhsT, W[:, l, k, 0:512], start=(k == 0), stop=(k == KC - 1))
                        o = nc.tensor.matmul(PS[:, 5 + 2 * b.q, 0:z_width(l) - 512], lhsT, W[:, l, k, 512:z_width(l)],
                                             start=(k == 0), stop=(k == KC - 1))
                    return o

                def first_half(b):
                    pe.wait_ge(s_xT, b.n + (NB * l + 1))
                    free_again(pe, b, s_zr, l)
                    product(b, range(KC // 2))

                def second_half(b):
                    product(b, range(KC // 2, KC)).then_inc(s_zp, 1)

                pe.wait_ge(s_waug, l + 1)
                if l:
                    pe.wait_ge(s_acc_free, 2 + NB * l)
                sweep_nodes(pe, [(first_half, 0), (turn_rows(l, lambda q: flat_banks(2 * q)), 1), (second_half, 0)])
                H = HEADS[l]
                pe.wait_ge(s_zr, NB * (l + 1))
                pe.wait_ge(s_tab, NB * (l + 1))
                nc.tensor.transpose(PS[0:H, 7, 0:P], gm[:, 0:H], ident[:, :]).then_inc(s_gmT, 1)
                pe.wait_ge(s_diag, l + 1)
                nc.tensor.matmul(PS[:, 7, P:P + H], ones[0:H, :], gmb[0:H, 0, 0:H], start=True, stop=True).then_inc(s_gmB, 1)

            def ffn_weights():
                for u in range(24):
                    if u < 12:
                        frm = lambda k: rows_buf(u % 2, 0)[:, k * P:(k + 1) * P]
                        pe.wait_ge(s_wld[u % 2], 16 * (u // 2 + 1))
                    else:
                        h, half = divmod(u - 12, 2)
                        frm = lambda k: wo_rows(h)[:, (half * 8 + k) * FH:(half * 8 + k + 1) * FH]
                        if half == 0:
                            pe.wait_ge(s_wol[h % 2], 16 * (h // 2 + 1))
                    if u >= 2:
                        pe.wait_ge(s_wcp, u - 1)
                    for k in range(6 if u < 12 else 8):
                        to = flat_banks(2 * (u % 2))[0:P if u < 12 else FH, k * P:(k + 1) * P]
                        o = nc.tensor.transpose(to, frm(k), ident[:, :])
                    o.then_inc(s_wT, 1)

            def edge_sweep(l):
                H = HEADS[l]
                for bank in range(4):
                    nc.tensor.matmul(PS[:, bank, :], zeros_h[:, 0:P], zeros_h[:, :], start=True, stop=True)

                def turn_S(g, jj):
                    pe.wait_ge(s_S, g + (NG * l + 1))
                    for j in range(G):
                        o = nc.tensor.transpose(flat_banks(4)[:, j * P:(j + 1) * P], S[:, jj, j, :], ident[:, :])
                    o.then_inc(s_STp, 1)

                def blocks_of(g):
                    return nc.values_load_multi_w_load_instructions(
                        b_g[0:1, bass.ds(g, 1), 0:G].rearrange("o g j -> o (g j)"), engines=[mybir.EngineType.PE],
                        min_val=0, max_val=NB - 1)[1]

                def er_of_edges(g, jj, blocks):
                    pe.wait_ge(s_ST, g + (NG * l + 1))
                    for j, b in enumerate(blocks):
                        o = nc.tensor.matmul(PS[:, 6, (jj * G + j) * 2 * H:(jj * G + j + 1) * 2 * H], ST[:, jj, j, :],
                                             erm_flat(l)[:, bass.ds(b * (2 * H), 2 * H)], start=True, stop=True)
                    o.then_inc(s_er, 1)

                def add_up(g, jj, j, b):
                    k = g * G + j
                    w = D + H
                    slot = jj * G + j
                    odd = (b + l) % 2
                    pe.wait_ge(s_msg, k + (V * l + 1))
                    pe.wait_ge(s_acc_free, b + (NB * l + 1))
                    flat = PS[:, :, :].rearrange("p b n -> p (b n)")
                    nc.tensor.matmul(flat[:, bass.ds(odd * 1024, HALF)], S[:, jj, j, :], arena[:, slot * w:slot * w + HALF],
                                     start=False, stop=True, skip_group_check=True)
                    nc.tensor.matmul(flat[:, bass.ds(odd * 1024 + 512, HALF + H)], S[:, jj, j, :],
                                     arena[:, slot * w + HALF:(slot + 1) * w],
                                     start=False, stop=True, skip_group_check=True).then_inc(s_agg, 1)

                def body(i, last):
                    now, then = blocks_of(NBUF * i), blocks_of(NBUF * i + 1)
                    for jj in range(NBUF):
                        g = NBUF * i + jj
                        if not (last and jj == NBUF - 1):
                            er_of_edges(g + 1, (jj + 1) % NBUF, then)
                        after = None
                        for j in range(G):
                            if j == 1 and not (last and jj >= NBUF - 2):
                                after = blocks_of(g + 2)
                            if j == G - 1 and not (last and jj >= NBUF - 2):
                                turn_S(g + 2, (jj + 2) % NBUF)
                            add_up(g, jj, j, now[j])
                        now, then = then, after

                pe.wait_ge(s_erm, l + 1)
                turn_S(0, 0)
                er_of_edges(0, 0, blocks_of(0))
                turn_S(1, 1)
                with pe.Fori(0, NI - 1) as i:
                    body(i, False)
                body(NI - 1, True)

            for l in range(3):
                node_sweep(l)
                if l == 2:
                    ffn_weights()
                    pe.wait_ge(s_wcp, 24)
                edge_sweep(l)

            turn = turn_rows(3, lambda q: flat_banks(0))
            pe.wait_ge(s_acc_free, 2 + NB * 3)
            pe.wait_ge(s_cload, 16 * 3)
            for k in range(KC):
                o = nc.tensor.transpose(PS[:, 2, k * EX:(k + 1) * EX], Wr_rows[:, k * P:(k + 1) * P], ident[0:EX, 0:EX])
            o.then_inc(s_wT, 1)
            pe.wait_ge(s_wcp, 25)

            def logits(b):
                pe.wait_ge(s_xT, b.n + (NB * 3 + 1))
                for k in range(KC):
                    o = nc.tensor.matmul(PS[:, 7, bass.ds(b.n * EX, EX)], xT(b.q)[:, k * P:(k + 1) * P],
                                         WrT[:, k * EX:(k + 1) * EX], start=(k == 0), stop=(k == KC - 1))
                o.then_inc(s_lg, 1)

            sweep_nodes(pe, [(turn, 1), (logits, 0)])

            pe.wait_ge(s_pairs, 1)
            pairs = routing("pairs")
            nc.tensor.matmul(PS[:, 4, 0:NB * EX], earlier[:, :], pairs, start=True, stop=True)
            nc.tensor.matmul(PS[:, 5, 0:NB * EX], ones[:, :], pairs, start=True, stop=True).then_inc(s_ranks, 1)
            pe.wait_ge(s_onehots, 1)
            for m in range(NB * TOP):
                o = nc.tensor.matmul(PS[:, 6, 0:NS], at_place()[:, m, :], at_slot()[:, m, :],
                                     start=(m == 0), stop=(m == NB * TOP - 1))
            o.then_inc(s_tokens_p, 1)
            pe.wait_ge(s_routed, 1)
            experts = [None, None, None]

            def turn_tokens(b):
                pe.wait_ge(s_xg[b.q], 16 * b.turn + 16)
                if b.reuse or b.n:
                    pe.wait_ge(s_xgT, b.n)
                for k in range(KC):
                    o = nc.tensor.transpose(flat_banks(0)[:, k * P:(k + 1) * P], in0(b.q)[:, k * P:(k + 1) * P],
                                            ident[:, :])
                o.then_inc(s_xgTp, 1)

            def up(b):
                if b.q == 0:
                    experts[:] = nc.values_load_multi_w_load_instructions(
                        expert_at[0:1, bass.ds(b.turn, 1), 0:3].rearrange("o s j -> o (s j)"),
                        engines=[mybir.EngineType.PE], min_val=0, max_val=EX - 1)[1]
                e = experts[1 + b.q]
                to = PS[:, 2, b.q * 256:b.q * 256 + FF]
                pe.wait_ge(s_xgT, b.n + 1)
                if b.reuse:
                    pe.wait_ge(s_gelu, b.n - 1)
                for k in range(KC):
                    nc.tensor.matmul(to, xT(b.q)[:, k * P:(k + 1) * P], WiT[:, k, bass.ds(e * FF, FF)],
                                     start=(k == 0), stop=False)
                nc.tensor.matmul(to, ones[0:1, :], bi_row[:, bass.ds(e * FF, FF)], start=False, stop=True).then_inc(s_up, 1)

            def down(b):
                e = experts[1] if b.q == 0 else experts[2] if b.fixed and b.n == NS - 1 else experts[0]
                pe.wait_ge(s_hT, b.n + 1)
                pe.wait_ge(s_y, b.n + 1)
                flat = WoT[:, :, :, :].rearrange("p e j d -> p (e j d)")
                for c, n in ((0, 512), (512, D - 512)):
                    to = flat_banks(4 + 2 * b.q)[:, c:c + n]
                    nc.tensor.matmul(to, hT(b.q)[0:FH, 0:P], flat[0:FH, bass.ds(e * (2 * D) + c, n)], start=True, stop=False)
                    o = nc.tensor.matmul(to, hT(b.q)[0:FH + 1, P:2 * P], flat[0:FH + 1, bass.ds(e * (2 * D) + (D + c), n)],
                                         start=False, stop=True)
                o.then_inc(s_down, 1)

            def turn_hidden(b):
                pe.wait_ge(s_gelu, b.n + 1)
                if b.reuse:
                    pe.wait_ge(s_hT, b.n - 1)
                for j in range(2):
                    o = nc.tensor.transpose(PS[0:FH, 3, (2 * b.q + j) * P:(2 * b.q + j + 1) * P],
                                            h_rows(b.q)[:, j * FH:(j + 1) * FH], ident[:, :])
                o.then_inc(s_hTp, 1)

            sweep_nodes(pe, [(up, 0), (turn_tokens, 1), (down, -1), (turn_hidden, 0)], count=NS)

        @block.vector
        def _(dve):
            dc = Chain(dve, s_dve)
            link = dc.link
            dve.wait_ge(s_const, 11)
            dst_f = arena[0:125, 0:400]
            link(nc.vector.tensor_copy(iota_row[:, :], iota_i[:, 0:P]))
            iota_f = arena[:, 10600:10600 + V]
            link(nc.vector.tensor_copy(iota_f, iota_i[:, :]))
            first = gate[:, 8:8 + NB - 1]
            link(nc.vector.tensor_scalar(first, iota_f[:, 0:NB - 1], float(P), float(P), ALU.mult, ALU.add))
            dve.wait_ge(s_dst, 16)
            dsti = S[:, :, :, :].rearrange("p a b c -> p (a b c)")[0:125, 0:400].bitcast(I32)
            dstf = S[:, :, :, :].rearrange("p a b c -> p (a b c)")[0:125, 400:800]
            link(nc.vector.tensor_copy(dstf, dsti))
            below = arena[0:125, 0:24 * 400].rearrange("p (b e) -> p b e", b=24)
            link(nc.vector.tensor_tensor(below, dstf.unsqueeze(1).broadcast_to([125, 24, 400]),
                                         first[0:125, :].unsqueeze(2).broadcast_to([125, 24, 400]), ALU.is_lt))
            nc.vector.tensor_reduce(wcount(), below, AX_X, ALU.add).then_inc(s_prep, 1)
            dve.wait_ge(s_cnt, 1)
            ti = wu[:, 0:2, :, :].rearrange("p a g h -> p (a g h)")[:, 0:NB - 1].bitcast(I32)
            link(nc.vector.tensor_copy(ti, PS[:, 0, 0:NB - 1]))
            link(nc.vector.tensor_scalar(ti, ti, 7, None, ALU.arith_shift_right))
            enter = gate[:, 8:8 + NB - 1]
            link(nc.vector.tensor_copy(enter, ti))
            link(nc.vector.tensor_scalar(enter, enter, float(ET - 1), None, ALU.min))
            link(nc.vector.scalar_tensor_tensor(out=enter, in0=iota_f[:, 0:NB - 1], scalar=1.0, in1=enter,
                                                op0=ALU.add, op1=ALU.add))
            for k0 in (0, V // 2):
                at = arena[:, 0:V // 2 * 24].rearrange("p (k b) -> p k b", b=24)
                link(nc.vector.tensor_tensor(at, iota_f[:, k0:k0 + V // 2].unsqueeze(2).broadcast_to([P, V // 2, 24]),
                                             enter.unsqueeze(1).broadcast_to([P, V // 2, 24]), ALU.is_ge))
                link(nc.vector.tensor_reduce(bk_f()[:, k0:k0 + V // 2], at, AX_X, ALU.add))
            link(nc.vector.tensor_tensor(tk_row(), iota_f[0:1, :], bk_f()[0:1, :], ALU.subtract))
            nc.vector.tensor_scalar(tk_row(), tk_row(), float(ET - 1), None, ALU.min).then_inc(s_prep, 1)
            link(nc.vector.tensor_copy(b_k[0:1, 0:V], bk_f()[0:1, :]))
            link(nc.vector.memset(b_k[0:1, V:V + 1], NB))
            starts = b_k[0:1, 0:V].rearrange("o (g j) -> o g j", j=G)
            link(nc.vector.tensor_copy(b_g[0:1, :, 0:G], starts))
            link(nc.vector.tensor_copy(b_g[0:1, :, 8:9], starts[:, :, 0:1]))
            link(nc.vector.tensor_copy(b_g[0:1, 0:NG - 1, 9:10], starts[:, 1:NG, 0:1]))
            link(nc.vector.memset(b_g[0:1, NG - 1:NG, 9:10], NB))
            link(nc.vector.tensor_copy(ends[0:1, 0:NB - 1], enter[0:1, :]))
            link(nc.vector.memset(ends[0:1, NB - 1:NB], V))
            dve.wait_ge(s_tk, 1)
            nc.vector.tensor_copy(gate[:, 0:3].bitcast(U32), PS[:, 1, 0:3]).then_inc(s_tki, 1)
            nc.vector.tensor_copy(gate[0:V - 3 * P, 3:4].bitcast(U32), PS[0:V - 3 * P, 1, 3:4]).then_inc(s_tki, 1)
            dve.wait_ge(s_rows_k, 16 * 4)
            nc.vector.tensor_copy(rows_f(), arena[:, 0:4 * 2 * P].bitcast(I32)).then_inc(s_rows_f, 1)
            dve.wait_ge(s_turned, 1)
            link(nc.vector.tensor_copy(src_k[:, :], PS[:, 2, 0:V]))
            link(nc.vector.scalar_tensor_tensor(out=dst_k[:, :], in0=bk_f(), scalar=-float(P), in1=PS[:, 3, 0:V],
                                                op0=ALU.mult, op1=ALU.add))
            nc.vector.memset(dst_k[:, ET + NB - 1:V], NO_NODE).then_inc(s_tables, 1)
            dve.wait_ge(s_tables, 1)
            nc.vector.tensor_copy(gate[:, 90:91], zeros[:, 0:1]).then_inc(s_prep, 1)

            for l in range(3):
                H = HEADS[l]
                dve.wait_ge(s_w[l], 16)
                dve.wait_ge(s_al, 32 * (l + 1))
                prod = arena[:, 7 * D:8 * D]
                for k in range(KC):
                    for j in range(2):
                        link(nc.vector.tensor_tensor(prod, W[:, l, k, 0:D], arena[:, (8 + j) * D:(9 + j) * D], ALU.mult))
                        link(nc.vector.tensor_reduce(W[:, l, k, D + j * H:D + (j + 1) * H],
                                                     prod.rearrange("p (h d) -> p h d", h=H), AX_X, ALU.add))
                nc.vector.tensor_copy(gate[:, 90:91], zeros[:, 0:1]).then_inc(s_al_used, 1)
            dve.wait_ge(s_al_used, 3)
            nc.vector.tensor_copy(gate[:, 91:92], zeros[:, 0:1]).then_inc(s_waug, 3)

            def in_ready(b, l):
                per = (1, 2, 2, 3)[l]
                uses = NB // 2 + 1 - b.q
                dve.wait_ge(s_in[b.q], 16 * per * b.turn + 16 * (per + uses * sum((1, 2, 2, 3)[:l])))

            def layernorm(b, rows, k, used):
                st = stats[:, b.q, :]
                nc.vector.bn_stats(st[:, 0:6], rows[:, 0:HALF])
                link(nc.vector.bn_stats(st[:, 6:12], rows[:, HALF:D]))
                dve.sem_inc(s_tick_dve)
                nc.vector.bn_aggr(st[:, 12:14], st[:, 0:12]).then_inc(s_stat, 1)
                dve.wait_ge(s_std, b.n + (NB * k + 1))
                link(nc.vector.reciprocal(st[:, 15:16], st[:, 14:15]))
                o = nc.vector.tensor_scalar(xr(b.q), rows, st[:, 12:13], st[:, 15:16], ALU.subtract, ALU.mult)
                return o

            def node_sweep(l):
                H = HEADS[l]

                def begin(b):
                    in_ready(b, l)
                    free_again(dve, b, s_xTp, l)
                    if l == 0:
                        link(layernorm(b, in0(b.q), 0, None))
                    else:
                        u, m = in0(b.q), in1(b.q)
                        link(nc.vector.tensor_tensor(u, u, m, ALU.add))
                        link(nc.vector.tensor_tensor(u, u, bias[:, :], ALU.add))
                        nc.vector.tensor_scalar(m, u, 0.0, None, ALU.min).then_inc(s_stat, 1)
                        dve.wait_ge(s_std, b.n + (NB * l + 1))
                        link(nc.vector.scalar_tensor_tensor(out=xr(b.q), in0=u, scalar=0.0, in1=m,
                                                            op0=ALU.max, op1=ALU.add))
                    dve.sem_inc(s_rows, 1)
                    dve.sem_inc(s_in_used, 1)

                def end(b):
                    dve.wait_ge(s_zr, b.n + (NB * l + 1))
                    nc.vector.tensor_copy(ert_flat(l)[:, bass.ds(b.n * H, H)], zr(b.q, D + 2 * H)[:, D + H:D + 2 * H])
                    link(nc.vector.tensor_tensor(gm[0:b.rows, 0:H], gm[0:b.rows, 0:H], zr(b.q, D + H)[0:b.rows, D:D + H],
                                                 ALU.max))
                    dve.sem_inc(s_tab, 1)

                link(nc.vector.memset(gm[:, :], -3.0e38))
                if l:
                    dve.wait_ge(s_bias, 16 * l)
                sweep_nodes(dve, [(begin, 2), (end, 0)], dc, 2 * (3 + 1))
                dve.wait_ge(s_gmT, l + 1)
                link(nc.vector.tensor_reduce(gmb[0:H, 1, 0:1], PS[0:H, 7, 0:P], AX_X, ALU.max))
                nc.vector.tensor_scalar(gmb[0:H, 0, 0:H], ident[0:H, 0:H], gmb[0:H, 1, 0:1], None,
                                        ALU.mult).then_inc(s_diag, 1)
                dve.wait_ge(s_gmB, l + 1)
                e3 = erm_flat(l).rearrange("p (b h) -> p b h", b=NB)
                ert3 = ert_flat(l).rearrange("p (b h) -> p b h", b=NB)
                link(nc.vector.tensor_copy(e3[:, :, 0:H], ert3))
                link(nc.vector.tensor_tensor(ert3, ert3, PS[:, 7, P:P + H].unsqueeze(1).broadcast_to([P, NB, H]), ALU.add))
                nc.vector.scalar_tensor_tensor(out=e3[:, :, H:2 * H], in0=ert3, scalar=SLOPE, in1=ert3,
                                               op0=ALU.mult, op1=ALU.max).then_inc(s_erm, 1)

            def edge_sweep(l):
                H = HEADS[l]
                w = D + H
                rows3 = arena[:, 0:U * w].rearrange("p (u n) -> p u n", u=U)

                def one_hots(g, jj):
                    dve.wait_ge(s_agg, G * g + (V * l + AHEAD - 2 * G))
                    to = dst_k[:, bass.ds(g * G, G)].unsqueeze(2).broadcast_to([P, G, P])
                    nc.vector.tensor_tensor(S[:, jj, :, :], iota_row[:, :].unsqueeze(1).broadcast_to([P, G, P]), to,
                                            ALU.is_equal).then_inc(s_S, 1)

                def exponents(g, i, jj):
                    dve.wait_ge(s_er, g + (NG * l + 1))
                    for j in range(jj * G, (jj + 1) * G):
                        dve.wait_ge(s_z[j], 16 * i + 16 * (NI * l + 1))
                    er = PS[:, 6, jj * G * 2 * H:(jj + 1) * G * 2 * H].rearrange("p (g h) -> p g h", g=G)
                    t, u = wt[:, jj, :, 0:H], wu[:, jj, :, 0:H]
                    link(nc.vector.tensor_tensor(u, edge_heads(l, jj), er[:, :, 0:H], ALU.add))
                    link(nc.vector.scalar_tensor_tensor(out=u, in0=u, scalar=SLOPE, in1=u, op0=ALU.mult, op1=ALU.max))
                    link(nc.vector.tensor_tensor(u, u, er[:, :, H:2 * H], ALU.subtract))
                    nc.vector.tensor_scalar(t, u, 0.0, None, ALU.min).then_inc(s_pre, 1)

                def weigh(g, jj):
                    dve.wait_ge(s_exp, g + (NG * l + 1))
                    for j in range(jj * G, (jj + 1) * G):
                        z = rows3[:, j, 0:D].rearrange("p (h d) -> p h d", h=H)
                        a = rows3[:, j, D:w].unsqueeze(2).broadcast_to([P, H, D // H])
                        nc.vector.tensor_tensor(z, z, a, ALU.mult).then_inc(s_msg, 1)

                def close_blocks(g):
                    lo = dve.value_load(b_k[0:1, bass.ds(g * G, 1)], min_val=0, max_val=NB)
                    hi = dve.value_load(b_k[0:1, bass.ds(g * G + G, 1)], min_val=0, max_val=NB)
                    with dve.If(lo < hi):
                        with dve.Fori(lo, hi) as b:
                            close(b)

                def close(b):
                    end = dve.value_load(ends[0:1, bass.ds(b, 1)], min_val=0, max_val=V)
                    dve.wait_ge(s_agg, end + (V * l + AHEAD))
                    odd = (b + l) % 2
                    flat = PS[:, :, :].rearrange("p b n -> p (b n)")
                    at = flat[:, bass.ds(odd * 1024, 1024)].rearrange("p (c n) -> p c n", c=2)
                    steps = []
                    den = at[:, 1, HALF:HALF + H]
                    nc.vector.tensor_scalar(rec[:, 0, 0:H], den, 0.5, None, ALU.max).then_inc(s_close, 1)
                    dve.wait_ge(s_close, b * 3 + (3 * NB * l + 1))
                    nc.vector.reciprocal(rec[:, 1, 0:H], rec[:, 0, 0:H]).then_inc(s_close, 1)
                    dve.wait_ge(s_close, b * 3 + (3 * NB * l + 2))
                    dve.wait_ge(s_sums_free, b + (NB * l + 1))
                    to = sums[:, :, :].rearrange("p q n -> p (q n)")[:, bass.ds(odd * D, D)]
                    for c in range(2):
                        hh = H // 2 if H > 1 else 1
                        r = rec[:, 1, c * hh:(c + 1) * hh] if H > 1 else rec[:, 1, 0:1]
                        o = nc.vector.tensor_tensor(
                            to[:, c * HALF:(c + 1) * HALF].rearrange("p (h d) -> p h d", h=hh),
                            at[:, c, 0:HALF].rearrange("p (h d) -> p h d", h=hh),
                            r.unsqueeze(2).broadcast_to([P, hh, HALF // hh]), ALU.mult)
                        o.then_inc(s_close if c == 0 else s_sums, 1)
                    dve.wait_ge(s_close, b * 3 + (3 * NB * l + 3))
                    dve.wait_ge(s_sums, b + (NB * l + 1))
                    dve.sem_inc(s_tick_dve)
                    nc.vector.tensor_copy(at[:, :, 0:HALF + H],
                                          zeros[:, 0:2 * (HALF + H)].rearrange("p (c n) -> p c n", c=2)).then_inc(s_acc_free, 1)

                def body(i, last):
                    for jj in range(NBUF):
                        g = NBUF * i + jj
                        exponents(g, i, jj)
                        if not (last and jj == NBUF - 1):
                            one_hots(g + 1, (jj + 1) % NBUF)
                        weigh(g, jj)
                        if jj or not isinstance(i, int) or i:
                            close_blocks(g - 1)

                one_hots(0, 0)
                body(0, False)
                with dve.Fori(1, NI - 1) as i:
                    dc.enter(i - 1, 3 * NBUF)
                    body(i, False)
                dc.leave(NI - 2)
                body(NI - 1, True)
                close_blocks(NG - 1)

            for l in range(3):
                node_sweep(l)
                edge_sweep(l)

            dve.wait_ge(s_wT, 25)
            nc.vector.tensor_copy(WrT[:, :], PS[:, 2, 0:KC * EX]).then_inc(s_wcp, 1)

            def begin(b):
                in_ready(b, 3)
                free_again(dve, b, s_xTp, 3)
                if b.reuse:
                    dve.wait_ge(s_kept[b.q], 16 * b.turn)
                    dve.wait_ge(s_kept_x2[b.q], 16 * b.turn)
                u = in0(b.q)
                link(nc.vector.tensor_tensor(u, u, in1(b.q), ALU.add))
                link(nc.vector.tensor_tensor(u, u, bias[:, :], ALU.add))
                link(nc.vector.tensor_tensor(x2(b.q), u, in2(b.q), ALU.add))
                link(layernorm(b, x2(b.q), 3, None))
                dve.sem_inc(s_rows, 1)
                dve.sem_inc(s_in_used, 1)

            dve.wait_ge(s_bias, 16 * 3)
            sweep_nodes(dve, [(begin, 2)], dc, 2 * 6)

            lg, pairs, t, best = routing("lg"), routing("pairs"), routing("t"), routing("best")
            one = [routing("one0"), routing("one1")]
            per_expert = lambda a: a.rearrange("p (b e) -> p b e", e=EX)
            over_blocks = lambda a: a.unsqueeze(1).broadcast_to([P, NB, EX])
            over_experts = lambda a: a.unsqueeze(2).broadcast_to([P, NB, EX])
            tt, ts = nc.vector.tensor_tensor, nc.vector.tensor_scalar
            dve.wait_ge(s_lg, NB)
            link(nc.vector.tensor_copy(lg, PS[:, 7, 0:NB * EX]))
            rising = routing("rising")
            link(ts(rising, iota_row[:, 0:EX], -1.0, float(EX), ALU.mult, ALU.add))
            token, real = routing("token"), routing("real")
            link(nc.vector.tensor_copy(token, token_i[:, :]))
            link(ts(real, token, float(N), None, ALU.is_lt))
            link(tt(token, token, real, ALU.mult))
            for j, v in enumerate((routing("v0"), routing("v1"))):
                link(nc.vector.tensor_reduce(v, per_expert(lg), AX_X, ALU.max))
                link(tt(per_expert(t), per_expert(lg), over_experts(v), ALU.is_equal))
                link(tt(per_expert(t), per_expert(t), over_blocks(rising), ALU.mult))
                link(nc.vector.tensor_reduce(best, per_expert(t), AX_X, ALU.max))
                link(tt(per_expert(one[j]), over_blocks(rising), over_experts(best), ALU.is_equal))
                if j == 0:
                    link(nc.vector.scalar_tensor_tensor(out=lg, in0=one[0], scalar=-3.0e38, in1=lg, op0=ALU.mult, op1=ALU.add))
            tt(routing("d"), routing("v1"), routing("v0"), ALU.subtract).then_inc(s_d, 1)
            for j in range(2):
                link(tt(per_expert(one[j]), per_expert(one[j]), over_experts(real), ALU.mult))
            tt(pairs, one[0], one[1], ALU.add).then_inc(s_pairs, 1)
            dve.wait_ge(s_e, 1)
            g0, g1 = routing("g0"), routing("g1")
            link(ts(t[:, 0:NB], routing("e"), 1.0, None, ALU.add))
            link(nc.vector.reciprocal(g0, t[:, 0:NB]))
            link(tt(g1, routing("e"), g0, ALU.mult))
            dve.wait_ge(s_ranks, 1)
            upto, other = routing("upto"), routing("other")
            link(nc.vector.tensor_copy(upto, PS[:, 5, 0:NB * EX]))
            n = 1
            while n < NB:
                link(nc.vector.tensor_copy(other[:, 0:n * EX], upto[:, 0:n * EX]))
                link(tt(other[:, n * EX:], upto[:, n * EX:], upto[:, 0:(NB - n) * EX], ALU.add))
                upto, other, n = other, upto, 2 * n
            slots, last_slot, swap = routing("slots"), routing("last_slot"), routing("swap")
            slots_i = routing("slots_i").bitcast(I32)
            link(ts(slots, upto[:, (NB - 1) * EX:], float(P - 1), None, ALU.add))
            link(nc.vector.tensor_copy(slots_i, slots))
            link(ts(slots_i, slots_i, 7, None, ALU.arith_shift_right))
            link(nc.vector.tensor_copy(slots, slots_i))
            link(nc.vector.tensor_copy(last_slot, slots))
            n = 1
            while n < EX:
                link(nc.vector.tensor_copy(swap[:, 0:n], last_slot[:, 0:n]))
                link(tt(swap[:, n:], last_slot[:, n:], last_slot[:, 0:EX - n], ALU.add))
                last_slot, swap, n = swap, last_slot, 2 * n
            link(tt(slots, last_slot, slots, ALU.subtract))
            link(tt(upto, upto, PS[:, 5, 0:NB * EX], ALU.subtract))
            link(tt(upto, upto, PS[:, 4, 0:NB * EX], ALU.add))
            link(nc.vector.scalar_tensor_tensor(out=per_expert(upto), in0=over_blocks(slots), scalar=float(P),
                                                in1=per_expert(upto), op0=ALU.mult, op1=ALU.add))
            place, slot = routing("place"), routing("slot")
            for j in range(2):
                link(tt(t, one[j], upto, ALU.mult))
                link(nc.vector.tensor_reduce(place.rearrange("p (b j) -> p b j", j=TOP)[:, :, j], per_expert(t), AX_X, ALU.add))
            flat_place = place_of[:, :, :].rearrange("p b j -> p (b j)")
            link(nc.vector.tensor_copy(flat_place, place))
            slot_i = t[:, 0:NB * TOP].bitcast(I32)
            link(ts(slot_i, flat_place, 7, None, ALU.arith_shift_right))
            link(nc.vector.tensor_copy(slot, slot_i))
            link(nc.vector.scalar_tensor_tensor(out=place, in0=slot, scalar=-float(P), in1=place, op0=ALU.mult, op1=ALU.add))
            for q in range(2):
                dve.wait_ge(s_kept[q], 16 * (NB // 2 + 1 - q))
                dve.wait_ge(s_kept_x2[q], 16 * (NB // 2 + 1 - q))
            link(tt(at_place(), iota_row[:, :].unsqueeze(1).broadcast_to([P, NB * TOP, P]),
                    place.unsqueeze(2).broadcast_to([P, NB * TOP, P]), ALU.is_equal))
            link(tt(at_slot(), iota_row[:, 0:NS].unsqueeze(1).broadcast_to([P, NB * TOP, NS]),
                    slot.unsqueeze(2).broadcast_to([P, NB * TOP, NS]), ALU.is_equal))
            tt(at_slot().rearrange("p (b j) s -> p b (j s)", j=TOP), at_slot().rearrange("p (b j) s -> p b (j s)", j=TOP),
               token.unsqueeze(2).broadcast_to([P, NB, TOP * NS]), ALU.mult).then_inc(s_onehots, 1)
            ended = ended_at()
            link(tt(ended, iota_row[0:1, 0:NS].unsqueeze(2).broadcast_to([1, NS, EX]),
                    last_slot[0:1, :].unsqueeze(1).broadcast_to([1, NS, EX]), ALU.is_ge))
            expert = routing("expert")[0:1, :]
            link(nc.vector.tensor_reduce(expert, ended, AX_X, ALU.add))
            link(ts(expert, expert, float(EX - 1), None, ALU.min))
            link(nc.vector.memset(expert_at[:, :, :], 0))
            two = expert.rearrange("o (i s) -> o i s", s=2)
            link(nc.vector.tensor_copy(expert_at[0:1, :, 1:3], two))
            link(nc.vector.tensor_copy(expert_at[0:1, 1:NS // 2, 0:1], two[:, 0:NS // 2 - 1, 1:2]))
            dve.wait_ge(s_tokens_p, 1)
            for q in range(2):
                link(nc.vector.memset(hT(q)[FH:FH + 1, :], 1.0))
            nc.vector.tensor_copy(token_of[:, :], PS[:, 6, 0:NS]).then_inc(s_routed, 1)

            def copy_y(b):
                dve.wait_ge(s_down, b.n + 1)
                dve.wait_ge(s_y_st[b.q], 16 * b.turn + 16)
                nc.vector.tensor_copy(zr(b.q, D), flat_banks(4 + 2 * b.q)[:, 0:D]).then_inc(s_y, 1)

            def copy_hT(b):
                dve.wait_ge(s_hTp, b.n + 1)
                if b.reuse:
                    dve.wait_ge(s_down, b.n - 1)
                nc.vector.tensor_copy(hT(b.q)[0:FH, :], PS[0:FH, 3, 2 * b.q * P:(2 * b.q + 2) * P]).then_inc(s_hT, 1)

            sweep_nodes(dve, [(copy_y, -1), (copy_hT, 0)], count=NS)

            def result(b):
                dve.wait_ge(s_x2in[b.q], 16 * b.turn + 16)
                dve.wait_ge(s_ab[b.q], 32 * b.turn + 32)
                if b.reuse:
                    dve.wait_ge(s_or_st[b.q], 16 * b.turn)
                dve.sem_inc(s_tick_dve)
                link(nc.vector.scalar_tensor_tensor(out=x2(b.q), in0=in0(b.q), scalar=g0[:, bass.ds(b.n, 1)], in1=x2(b.q),
                                                    op0=ALU.mult, op1=ALU.add))
                nc.vector.scalar_tensor_tensor(out=zr(b.q, D), in0=in1(b.q), scalar=g1[:, bass.ds(b.n, 1)], in1=x2(b.q),
                                               op0=ALU.mult, op1=ALU.add).then_inc(s_or, 1)

            sweep_nodes(dve, [(result, 0)], dc, 2)


_INS = ["x", "src", "dst"] + [f"L0_gnn_{n}{i}" for i in range(3) for n in ("W", "al", "ar", "b")] + [
    f"L0_ffn_{n}" for n in ("Wr", "Wi", "bi", "Wo", "bo")]


def kernel(**inputs):
    import numpy as _np
    import concourse.bacc as _bacc
    from concourse.bass_utils import run_bass_kernel_spmd as _run

    nc = _bacc.Bacc("TRN2", target_bir_lowering=False, num_devices=1)
    arrays, args = {}, {}
    for name in _INS:
        a = _np.ascontiguousarray(inputs[name])
        arrays[f"in_{name}"] = a
        args[name] = nc.dram_tensor(f"in_{name}", a.shape, mybir.dt.from_np(a.dtype), kind="ExternalInput").ap()
    out = nc.dram_tensor("out_0", (N, D), F32, kind="ExternalOutput").ap()
    gnn = [{n: args[f"L0_gnn_{n}{i}"] for n in ("W", "al", "ar", "b")} for i in range(3)]
    ffn = {n: args[f"L0_ffn_{n}"] for n in ("Wr", "Wi", "bi", "Wo", "bo")}
    gnn_ffn(nc, args["x"], args["src"], args["dst"], gnn, ffn, out)
    r = _run(nc, [arrays], core_ids=[0])
    return r.results[0]["out_0"]
```
